# Optimizing a Trainium2 kernel written in Bass

```python
import numpy as np
import jax
import jax.numpy as jnp

def _softmax(x, axis=-1):
    return jax.nn.softmax(x, axis=axis)

def _gelu(x):
    return jax.nn.gelu(x, approximate=True)

def _silu(x):
    return jax.nn.silu(x)

def _sigmoid(x):
    return jax.nn.sigmoid(x)

def _layernorm(x, axis=-1, eps=1e-05):
    m = jnp.mean(x, axis=axis, keepdims=True)
    v = jnp.var(x, axis=axis, keepdims=True)
    return (x - m) / jnp.sqrt(v + eps)

def _scatter_add(tgt, idx, src, axis=0):
    return tgt.at[idx].add(src)

def _segment_sum(src, seg, n):
    return jax.ops.segment_sum(src, seg, n)
kernel_name = 'mk_vit_tower_d1_tok_img512_r4_0fbce1'

def setup_inputs(seed: int=0):
    np.random.seed(seed)
    _w = jnp.asarray

    def _rec_inputs():
        import jax
        import jax.numpy as jnp
        _rk = jax.random.key(seed)
        x = -0.000372384 + 0.999952 * jax.random.normal(jax.random.fold_in(_rk, 1), (16, 128, 60, 108), jnp.float32)
        return x
    x = _rec_inputs()

    def _L0_tok_setup():
        import jax, jax.numpy as jnp
        import numpy as np
        CHANNEL = 128
        HIDDEN = 128
        KH, KW = (7, 7)
        SH, SW = (3, 3)
        PH, PW = (3, 3)
        C_IN = KH * KW * CHANNEL

        def unfold(x, kh, kw, sh, sw, ph, pw):
            B, C, H, W = x.shape
            xp = jnp.pad(x, ((0, 0), (0, 0), (ph, ph), (pw, pw)))
            Ho = (H + 2 * ph - kh) // sh + 1
            Wo = (W + 2 * pw - kw) // sw + 1
            ih = (jnp.arange(Ho) * sh)[:, None] + jnp.arange(kh)[None, :]
            iw = (jnp.arange(Wo) * sw)[:, None] + jnp.arange(kw)[None, :]
            patches = xp[:, :, ih[:, None, :, None], iw[None, :, None, :]]
            patches = patches.transpose(0, 2, 3, 1, 4, 5)
            return patches.reshape(B, Ho * Wo, C * kh * kw)
        key = jax.random.key(seed)
        kx, kw_, kb = jax.random.split(key, 3)
        x = jax.random.normal(kx, (16, CHANNEL, 60, 108), dtype=jnp.float32)
        bound = 1.0 / np.sqrt(C_IN)
        W = jax.random.uniform(kw_, (HIDDEN, C_IN), minval=-bound, maxval=bound, dtype=jnp.float32)
        b = jax.random.uniform(kb, (HIDDEN,), minval=-bound, maxval=bound, dtype=jnp.float32)
        return {'x': x, 'W': W, 'b': b}
    _L0_tok_all = _L0_tok_setup()
    _L0_tok_in = {k: v for k, v in _L0_tok_all.items() if k in ('W', 'b')}
    del _L0_tok_all

    def _L0_attn_setup():
        import jax, jax.numpy as jnp
        import numpy as np
        B, L, C = (4, 512, 128)
        H = 8
        HD = C // H

        def _rope_tables(seq_len, dim, dtype):
            inv_freq = 1.0 / 10000.0 ** (jnp.arange(0, dim, 2, dtype=jnp.float32) / dim)
            pos = jnp.arange(seq_len, dtype=jnp.float32)
            sinusoid = pos[:, None] * inv_freq[None, :]
            sin = jnp.sin(sinusoid).astype(dtype)[None, :, None, :]
            cos = jnp.cos(sinusoid).astype(dtype)[None, :, None, :]
            return (cos, sin)

        def _rotate_half(x):
            x1, x2 = jnp.split(x, 2, axis=-1)
            return jnp.concatenate([-x2, x1], axis=-1)
        key = jax.random.key(seed)
        ks = jax.random.split(key, 5)
        s = 0.02
        return {'x': jax.random.normal(ks[0], (B, L, C), dtype=jnp.float32), 'qkv_w': jax.random.normal(ks[1], (3 * C, C), dtype=jnp.float32) * s, 'qkv_b': jax.random.normal(ks[2], (3 * C,), dtype=jnp.float32) * s, 'out_w': jax.random.normal(ks[3], (C, C), dtype=jnp.float32) * s, 'out_b': jax.random.normal(ks[4], (C,), dtype=jnp.float32) * s}
    _L0_attn_all = _L0_attn_setup()
    _L0_attn_in = {k: v for k, v in _L0_attn_all.items() if k in ('qkv_w', 'qkv_b', 'out_w', 'out_b')}
    del _L0_attn_all

    def _L0_ffn_setup():
        import jax, jax.numpy as jnp
        import numpy as np
        B, S, D, H, E = (4, 512, 128, 8, 8)
        FF = 4 * D
        HD = D // H
        EPS = 1e-05

        def _layernorm(x, g, b):
            mu = jnp.mean(x, axis=-1, keepdims=True)
            var = jnp.mean((x - mu) ** 2, axis=-1, keepdims=True)
            return (x - mu) * jax.lax.rsqrt(var + EPS) * g + b
        key = jax.random.key(seed)
        ks = jax.random.split(key, 16)
        s = 0.02
        return {'x': jax.random.normal(ks[0], (B, S, D), dtype=jnp.float32), 'ln1_g': jnp.ones((D,), jnp.float32), 'ln1_b': jnp.zeros((D,), jnp.float32), 'Wq': jax.random.normal(ks[1], (D, D), jnp.float32) * s, 'bq': jnp.zeros((D,), jnp.float32), 'Wk': jax.random.normal(ks[2], (D, D), jnp.float32) * s, 'bk': jnp.zeros((D,), jnp.float32), 'Wv': jax.random.normal(ks[3], (D, D), jnp.float32) * s, 'bv': jnp.zeros((D,), jnp.float32), 'Wo': jax.random.normal(ks[4], (D, D), jnp.float32) * s, 'bo': jnp.zeros((D,), jnp.float32), 'gate_W': jax.random.normal(ks[5], (D, E), jnp.float32) * s, 'gate_b': jnp.zeros((E,), jnp.float32), 'W1': jax.random.normal(ks[6], (E, D, FF), jnp.float32) * s, 'b1': jnp.zeros((E, FF), jnp.float32), 'W2': jax.random.normal(ks[7], (E, FF, D), jnp.float32) * s, 'b2': jnp.zeros((E, D), jnp.float32)}
    _L0_ffn_all = _L0_ffn_setup()
    _L0_ffn_in = {k: v for k, v in _L0_ffn_all.items() if k in ('ln1_g', 'ln1_b', 'Wq', 'bq', 'Wk', 'bk', 'Wv', 'bv', 'Wo', 'bo', 'gate_W', 'gate_b', 'W1', 'b1', 'W2', 'b2')}
    del _L0_ffn_all
    return {'x': x, 'L0_tok_W': _L0_tok_in['W'], 'L0_tok_b': _L0_tok_in['b'], 'L0_attn_qkv_w': _L0_attn_in['qkv_w'], 'L0_attn_qkv_b': _L0_attn_in['qkv_b'], 'L0_attn_out_w': _L0_attn_in['out_w'], 'L0_attn_out_b': _L0_attn_in['out_b'], 'L0_ffn_ln1_g': _L0_ffn_in['ln1_g'], 'L0_ffn_ln1_b': _L0_ffn_in['ln1_b'], 'L0_ffn_Wq': _L0_ffn_in['Wq'], 'L0_ffn_bq': _L0_ffn_in['bq'], 'L0_ffn_Wk': _L0_ffn_in['Wk'], 'L0_ffn_bk': _L0_ffn_in['bk'], 'L0_ffn_Wv': _L0_ffn_in['Wv'], 'L0_ffn_bv': _L0_ffn_in['bv'], 'L0_ffn_Wo': _L0_ffn_in['Wo'], 'L0_ffn_bo': _L0_ffn_in['bo'], 'L0_ffn_gate_W': _L0_ffn_in['gate_W'], 'L0_ffn_gate_b': _L0_ffn_in['gate_b'], 'L0_ffn_W1': _L0_ffn_in['W1'], 'L0_ffn_b1': _L0_ffn_in['b1'], 'L0_ffn_W2': _L0_ffn_in['W2'], 'L0_ffn_b2': _L0_ffn_in['b2']}

def reference(x, L0_tok_W, L0_tok_b, L0_attn_qkv_w, L0_attn_qkv_b, L0_attn_out_w, L0_attn_out_b, L0_ffn_ln1_g, L0_ffn_ln1_b, L0_ffn_Wq, L0_ffn_bq, L0_ffn_Wk, L0_ffn_bk, L0_ffn_Wv, L0_ffn_bv, L0_ffn_Wo, L0_ffn_bo, L0_ffn_gate_W, L0_ffn_gate_b, L0_ffn_W1, L0_ffn_b1, L0_ffn_W2, L0_ffn_b2):
    import jax
    import jax.numpy as jnp

    def _L0_tok_ref(x, W, b):
        import jax, jax.numpy as jnp
        import numpy as np
        CHANNEL = 128
        HIDDEN = 128
        KH, KW = (7, 7)
        SH, SW = (3, 3)
        PH, PW = (3, 3)
        C_IN = KH * KW * CHANNEL

        def unfold(x, kh, kw, sh, sw, ph, pw):
            B, C, H, W = x.shape
            xp = jnp.pad(x, ((0, 0), (0, 0), (ph, ph), (pw, pw)))
            Ho = (H + 2 * ph - kh) // sh + 1
            Wo = (W + 2 * pw - kw) // sw + 1
            ih = (jnp.arange(Ho) * sh)[:, None] + jnp.arange(kh)[None, :]
            iw = (jnp.arange(Wo) * sw)[:, None] + jnp.arange(kw)[None, :]
            patches = xp[:, :, ih[:, None, :, None], iw[None, :, None, :]]
            patches = patches.transpose(0, 2, 3, 1, 4, 5)
            return patches.reshape(B, Ho * Wo, C * kh * kw)
        feat = unfold(x, KH, KW, SH, SW, PH, PW)
        feat = jnp.einsum('blc,hc->blh', feat, W) + b
        return feat

    def _L0_attn_ref(x, qkv_w, qkv_b, out_w, out_b):
        import jax, jax.numpy as jnp
        import numpy as np
        B, L, C = (4, 512, 128)
        H = 8
        HD = C // H

        def _rope_tables(seq_len, dim, dtype):
            inv_freq = 1.0 / 10000.0 ** (jnp.arange(0, dim, 2, dtype=jnp.float32) / dim)
            pos = jnp.arange(seq_len, dtype=jnp.float32)
            sinusoid = pos[:, None] * inv_freq[None, :]
            sin = jnp.sin(sinusoid).astype(dtype)[None, :, None, :]
            cos = jnp.cos(sinusoid).astype(dtype)[None, :, None, :]
            return (cos, sin)

        def _rotate_half(x):
            x1, x2 = jnp.split(x, 2, axis=-1)
            return jnp.concatenate([-x2, x1], axis=-1)
        b, l, c = x.shape
        hd = c // H
        qkv = x @ qkv_w.T + qkv_b
        q, k, v = jnp.split(qkv, 3, axis=-1)
        q = q.reshape(b, l, H, hd)
        k = k.reshape(b, l, H, hd)
        v = v.reshape(b, l, H, hd)
        cos, sin = _rope_tables(l, hd, x.dtype)
        q1, q2 = (q[..., :hd // 2], q[..., hd // 2:])
        k1, k2 = (k[..., :hd // 2], k[..., hd // 2:])
        q1r = q1 * cos + _rotate_half(q1) * sin
        k1r = k1 * cos + _rotate_half(k1) * sin
        q2r = q2 * cos + _rotate_half(q2) * sin
        k2r = k2 * cos + _rotate_half(k2) * sin
        q = jnp.concatenate([q1r, q2r], axis=-1)
        k = jnp.concatenate([k1r, k2r], axis=-1)
        scale = 1.0 / jnp.sqrt(jnp.asarray(hd, dtype=x.dtype))
        scores = jnp.einsum('bqhd,bkhd->bhqk', q, k) * scale
        weights = jax.nn.softmax(scores, axis=-1)
        attn = jnp.einsum('bhqk,bkhd->bqhd', weights, v).reshape(b, l, c)
        return attn @ out_w.T + out_b

    def _L0_ffn_ref(x, ln1_g, ln1_b, Wq, bq, Wk, bk, Wv, bv, Wo, bo, gate_W, gate_b, W1, b1, W2, b2):
        import jax, jax.numpy as jnp
        import numpy as np
        B, S, D, H, E = (4, 512, 128, 8, 8)
        FF = 4 * D
        HD = D // H
        EPS = 1e-05

        def _layernorm(x, g, b):
            mu = jnp.mean(x, axis=-1, keepdims=True)
            var = jnp.mean((x - mu) ** 2, axis=-1, keepdims=True)
            return (x - mu) * jax.lax.rsqrt(var + EPS) * g + b
        b, s, d = x.shape
        q = (x @ Wq + bq).reshape(b, s, H, HD)
        k = (x @ Wk + bk).reshape(b, s, H, HD)
        v = (x @ Wv + bv).reshape(b, s, H, HD)
        scores = jnp.einsum('bqhd,bkhd->bhqk', q, k) / jnp.sqrt(jnp.float32(HD))
        attn = jax.nn.softmax(scores, axis=-1)
        o = jnp.einsum('bhqk,bkhd->bqhd', attn, v).reshape(b, s, d) @ Wo + bo
        h = _layernorm(x + o, ln1_g, ln1_b)
        t = h.reshape(b * s, d)
        probs = jax.nn.softmax(t @ gate_W + gate_b, axis=-1)
        idx = jnp.argmax(probs, axis=-1)
        gw = jnp.max(probs, axis=-1)
        hid = jax.nn.gelu(jnp.einsum('nd,edf->enf', t, W1) + b1[:, None, :])
        out_all = jnp.einsum('enf,efd->end', hid, W2) + b2[:, None, :]
        onehot = jax.nn.one_hot(idx, E, dtype=t.dtype)
        out = jnp.einsum('ne,end->nd', onehot, out_all)
        out = out * gw[:, None]
        return out.reshape(b, s, d)
    h = _L0_tok_ref(x, L0_tok_W, L0_tok_b)
    h = h + _L0_attn_ref(_layernorm(h, axis=-1), L0_attn_qkv_w, L0_attn_qkv_b, L0_attn_out_w, L0_attn_out_b)
    h = h + _L0_ffn_ref(_layernorm(h, axis=-1), L0_ffn_ln1_g, L0_ffn_ln1_b, L0_ffn_Wq, L0_ffn_bq, L0_ffn_Wk, L0_ffn_bk, L0_ffn_Wv, L0_ffn_bv, L0_ffn_Wo, L0_ffn_bo, L0_ffn_gate_W, L0_ffn_gate_b, L0_ffn_W1, L0_ffn_b1, L0_ffn_W2, L0_ffn_b2)
    return h

_drawn_inputs = setup_inputs


def setup_inputs(seed=0):
    import zlib

    import numpy as np

    out = dict(_drawn_inputs(seed))
    spreads = {'L0_ffn_ln1_g': (1.0, 0.6),
     'L0_ffn_ln1_b': (0.0, 0.725),
     'L0_ffn_bq': (0.0, 0.8),
     'L0_ffn_bk': (0.0, 2.0),
     'L0_ffn_bv': (0.0, 0.8),
     'L0_ffn_bo': (0.0, 0.8),
     'L0_ffn_gate_b': (0.0, 0.274),
     'L0_ffn_b1': (0.0, 0.8),
     'L0_ffn_b2': (0.0, 0.523)}
    factors = {'L0_tok_b': 4.216,
     'L0_attn_qkv_w': 8.0,
     'L0_attn_qkv_b': 5.781,
     'L0_attn_out_w': 5.432,
     'L0_ffn_Wq': 8.0,
     'L0_ffn_Wk': 8.0,
     'L0_ffn_Wv': 8.0,
     'L0_ffn_Wo': 8.0,
     'L0_ffn_W1': 3.033,
     'L0_ffn_W2': 2.763}
    for name, (base, spread) in spreads.items():
        noise = np.random.default_rng([zlib.crc32(name.encode()), seed]).standard_normal(out[name].shape)
        drawn = base * np.exp(spread * noise) if base else spread * noise
        out[name] = jnp.asarray(drawn.astype(out[name].dtype))
    for name, factor in factors.items():
        out[name] = (out[name] * factor).astype(out[name].dtype)
    return out
```

```python
from contextlib import ExitStack

import numpy as np

import concourse.bass as bass
from concourse import mybir

F32 = mybir.dt.float32
F32R = mybir.dt.float32r
BF16 = mybir.dt.bfloat16
U16 = mybir.dt.uint16
ALU = mybir.AluOpType
ACT = mybir.ActivationFunctionType
AX = mybir.AxisListType

B, C, HI, WI = 16, 128, 60, 108
KH, STRIDE, PAD = 7, 3, 3
HO, WO = (HI + 2 * PAD - KH) // STRIDE + 1, (WI + 2 * PAD - KH) // STRIDE + 1
TAPS = KH * KH
L = HO * WO
HL = L // 2
H, HD = 8, C // 8
KB = 120
NB = L // KB
GH = 4
NG = H // GH
ATT = 2
STEPS = 2 * NB
GROWS = GH * NB
TILES = 2 * GROWS
AHEAD = 8
PER_STEP = 5
ROWS1_STEP = 10
PAIRS = ATT * NG * STEPS * 2
NP = 4
OUTS = ATT * NG * 2
E, FF = 8, 4 * C
FB = FF // C
EPS = 1e-5
SCALE = 1.0 / float(HD) ** 0.5

HROWS = HO // 2
XROWS = 37
XCOLS = (WI + 2 * PAD) // STRIDE
ROW0 = (0, 27)
BASE = (0, PAD)
CHUNKS = (((0, 11), (11, 10), (21, 10)), ((27, 11), (38, 11), (49, 11)))
CH = 3
CPI = 2 * CH
RAW_ROWS = 11
BIG_TAPS = 40

TERMS = ((0, 0), (0, 1), (1, 0), (1, 1), (0, 2), (2, 0))
SROWS = HD * len(TERMS)
MAXROW = C - 3
STACK_IN = 16 * len(TERMS)


def slot_uses():
    u = []
    for a in range(ATT):
        u += [f"mean{a}", f"var{a}"] + (["q0", "qp0", "k0", "kp0", "v0"] if a == 0 else ["q1", "k1", "v1"])
        u += [f"max{a}.{n}" for n in range(GROWS)] + [f"rows{a}0"]
        for g in range(NG):
            for s in range(STEPS):
                u += [f"s{a}{g}.{s}.{pair}" for pair in range(2)]
                if (g, s) == (0, ROWS1_STEP):
                    u += [f"rows{a}1"]
        u += [f"out{a}"]
    u += ["mean2", "var2", "gate"]
    for e in range(E):
        for f in range(FB):
            u += [f"h{e}.{f}"]
            if (e, f) == (0, 1):
                u += ["onehot", "weight"]
            if f == 2 and e + 1 < E:
                u += [f"mask{e + 1}"]
    return u + ["gw", "b2"]


T_INDEX = {name: n for n, name in enumerate(slot_uses())}
assert len(T_INDEX) % 2 == 0
T_PER = len(T_INDEX) // 2


def slot(use):
    return T_INDEX[use] % 2


def filled(i, use):
    return i * T_PER + (T_INDEX[use] // 2 + 1)


def before(i, use):
    return i * T_PER + T_INDEX[use] // 2


def pair_no(a, g, s, pair):
    return ((a * NG + g) * STEPS + s) * 2 + pair


LOADS = {
    "mean_w": [C, C], "ident": [C, C], "cos": [C, L], "sin": [C, L], "key": [KB, NB, E], "ones8": [E, C],
    "vecs": [C, 12], "b1": [C, E * FB], "q0": [C, C], "qp0": [C, C], "k0": [C, C], "kp0": [C, C], "v0": [C, C],
    "q1": [C, C], "k1": [C, C], "v1": [C, C], "bv0": [KB, C], "bv1": [KB, C],
    "o0": [C, NG, C], "o1": [C, NG, C], "gate_w": [C, E], "gate_b": [KB, NB, E],
    "w1": [C, E * FF], "w2": [C, E * FB, C], "b2": [E, C],
}
VEC = {n: k for k, n in enumerate(
    ["conv_b", "q0", "qp0", "k0", "kp0", "q1", "k1", "o0", "o1", "ln_g", "ln_b", "eps"])}

FILL = ({"mean": 3, "var": 4, "split": 18, "tiles": 10, "rows0": 7, "rows1": TAPS},
        {"mean": 3, "var": 4, "split": 18, "tiles": 0, "rows0": 7, "rows1": 3, "out": 5},
        {"mean": 4, "var": TAPS})


def build(nc, x, w_conv, sel_rows, consts, out):
    with ExitStack() as ctx:
        def sb(name, shape, dt=F32):
            return ctx.enter_context(nc.sbuf_tensor(name, shape, dt))

        def psum(name, shape):
            return ctx.enter_context(nc.psum_tensor(name, shape, F32))

        def sem(name):
            return ctx.enter_context(nc.semaphore(name))

        T = [psum(f"T{s}", [128, 2, 512]) for s in range(2)]
        M = psum("M", [128, 2, 512])
        O = psum("O", [128, 512])
        CV = psum("CV", [128, 512])

        def halves(ap):
            return ap.rearrange("p (a b) -> p a b", a=2)

        def tv(use):
            return T[slot(use)][:, :, 0:HL]

        wch, wcl = sb("wch", [C, TAPS, C], F32R), sb("wcl", [C, TAPS, C], F32R)
        K = {name: sb(name, shape) for name, shape in LOADS.items()}
        selb = sb("selb", [E, E, C], BF16)

        def vec(name):
            return K["vecs"][:, VEC[name]:VEC[name] + 1]

        raw = [sb(f"raw{n}", [C, RAW_ROWS, WI]) for n in range(2)]
        xh = sb("xh", [C, XROWS, STRIDE, XCOLS], F32R)
        xl = sb("xl", [C, XROWS, STRIDE, XCOLS], F32R)
        hc, h1, nx = sb("hc", [C, L]), sb("h1", [C, L]), sb("nx", [C, L])
        xc, sq = sb("xc", [C, L]), sb("sq", [C, L])
        qk = sb("qk", [C, 2, L])
        parts = sb("parts", [C, 6, L], BF16)
        V = sb("V", [KB, NB, H, 32])
        rm2, rm = sb("rm2", [KB, GROWS, 2]), sb("rm", [KB, NG * GROWS])
        rmt, rmp = sb("rmt", [GROWS, KB]), sb("rmp", [GROWS, 3, KB], BF16)
        gt, gs = sb("gt", [KB, 6, NB, E]), sb("gs", [KB, 4, NB])
        onehotT, weightT = sb("onehotT", [E, L], BF16), sb("weightT", [E, L])
        P = [parts[:, 2 * n:2 * n + 2, :].rearrange("p a b -> p (a b)").bitcast(F32)[0:KB, :].rearrange(
            "p (j q) -> p j q", j=2) for n in range(3)] + [sq[0:KB, :].rearrange("p (j q) -> p j q", j=2)]
        big = sb("big", [128, H * 2 * L], BF16)
        stack = big[:, :].rearrange("p (s h n) -> p s h n", h=H, s=2)
        bigf = big[:, :].bitcast(F32)
        tok = bigf[:, 0:L]
        hid = [bigf[:, (1 + n) * L:(2 + n) * L] for n in range(3)]
        sel = bigf[:, 4 * L:5 * L]
        mask = [big[:, (10 + n) * L:(11 + n) * L] for n in range(2)]
        o_sb, sums = xc[:, 0:HL], xc[:, HL:L]
        on = [qk[:, g, :] for g in range(NG)]

        conv_w_loaded, consts_loaded = sem("conv_w_loaded"), sem("consts_loaded")
        weights_split, cleared = sem("weights_split"), sem("cleared")
        t_full, t_read = [sem(f"t_full{s}") for s in range(2)], [sem(f"t_read{s}") for s in range(2)]
        m_full, m_read = [sem(f"m_full{s}") for s in range(2)], [sem(f"m_read{s}") for s in range(2)]
        o_read = sem("o_read")
        conv_full, conv_read = sem("conv_full"), sem("conv_read")
        raw_in = [sem(f"raw_in{n}") for n in range(2)]
        x_high, x_split = sem("x_high"), sem("x_split")
        sq_ready, log_ready, rstd_ready, n_ready = sem("sq_ready"), sem("log_ready"), sem("rstd_ready"), sem("n_ready")
        rope_ready = sem("rope_ready")
        high_ready, rest_ready, mid_ready, low_ready = (sem(f"{n}_ready") for n in ("high", "rest", "mid", "low"))
        ones_ready = sem("ones_ready")
        stacked = [sem(f"stacked{h}") for h in range(H)]
        rowmax_ready, rowmax_part, rowmax_in = sem("rowmax_ready"), sem("rowmax_part"), sem("rowmax_in")
        pv_done = sem("pv_done")
        sums_ready, inverse_ready, on_ready = sem("sums_ready"), sem("inverse_ready"), sem("on_ready")
        tok_ready = sem("tok_ready")
        gate_step, gate_exp = sem("gate_step"), sem("gate_exp")
        down_done, acc_read = sem("down_done"), sem("acc_read")
        y_ready, stored = sem("y_ready"), sem("stored")

        held = {nc.vector.engine: sem("held_vector"), nc.gpsimd.engine: sem("held_gpsimd")}

        ALL_CONSTS = 16 * (len(LOADS) + 1)

        def hold(eng):
            eng.sem_inc(held[eng.engine], 1)

        def every_image(eng, body):
            body(0, True, True)
            with eng.Fori(1, B - 2) as i:
                body(i, True, True)
            body(B - 2, True, False)
            body(B - 1, False, False)

        block = ctx.enter_context(nc.Block())

        @block.sync
        def _(sp):
            def load_rows(m, half, chunks=range(CH)):
                for c in chunks:
                    row0, rows = CHUNKS[half][c]
                    n, b = CH * half + c, (CH * half + c) % 2
                    if not (isinstance(m, int) and CPI * m + n < 2):
                        sp.wait_ge(x_split, m * CPI + (n - 1))
                    sp.dma_start(raw[b][:, 0:rows, :], x[m, :, row0:row0 + rows, :]).then_inc(raw_in[b], 16)

            load_rows(0, 0)
            sp.dma_start(bigf[:, 0:BIG_TAPS * C].rearrange("p (t n) -> p t n", n=C),
                         w_conv[:, 0:BIG_TAPS, :]).then_inc(conv_w_loaded, 16)
            sp.dma_start(qk[:, :, :].rearrange("p a b -> p (a b)")[:, 0:(TAPS - BIG_TAPS) * C].rearrange(
                "p (t n) -> p t n", n=C), w_conv[:, BIG_TAPS:TAPS, :]).then_inc(conv_w_loaded, 16)
            for name in LOADS:
                sp.dma_start(K[name][:], consts[name]).then_inc(consts_loaded, 16)
            sp.dma_start(parts[:, :, :].rearrange("p a b -> p (a b)").bitcast(F32)[0:E, 0:E * C],
                         sel_rows).then_inc(consts_loaded, 16)
            load_rows(0, 1)
            load_rows(1, 0)

            def stack_heads(i, a):
                sp.wait_ge(low_ready, i * 2 * ATT + (2 * a + 2))
                for h in range(H):
                    for r, (qp, kp) in enumerate(TERMS):
                        sp.dma_start(stack[HD * r:HD * (r + 1), :, h, :],
                                     parts[HD * h:HD * (h + 1), qp:4 + kp:3 + kp - qp, :]).then_inc(stacked[h], 16)

            def body(i, next_conv, load_ahead):
                if next_conv:
                    load_rows(i + 1, 1, range(CH - 1))
                sp.wait_ge(stored, i * 16)
                stack_heads(i, 0)
                if next_conv:
                    load_rows(i + 1, 1, [CH - 1])
                if load_ahead:
                    load_rows(i + 2, 0, range(CH - 1))
                stack_heads(i, 1)
                if load_ahead:
                    load_rows(i + 2, 0, [CH - 1])
                sp.wait_ge(y_ready, i + 1)
                sp.dma_start(out[i], sel).then_inc(stored, 16)

            every_image(sp, body)
            sp.wait_ge(stored, B * 16)

        @block.tensor
        def _(pe):
            def mm(out_ap, lhsT, rhs, start=True, stop=True, **kw):
                return nc.tensor.matmul(out_ap, lhsT, rhs, start=start, stop=stop, skip_group_check=True, **kw)

            def project(i, use, w, src):
                pe.wait_ge(t_read[slot(use)], before(i, use))
                for hf in range(2):
                    last = mm(T[slot(use)][0:w.shape[-1], hf, 0:HL], w, src[:, hf * HL:(hf + 1) * HL])
                last.then_inc(t_full[slot(use)], 1)

            def conv_tap(m, half, tap):
                if tap == 0:
                    pe.wait_ge(x_split, m * CPI + CH * (half + 1))
                    pe.wait_ge(conv_read, m * 2 + half)
                kh, kw = divmod(tap, KH)
                r0 = BASE[half] + kh

                def window(t):
                    return t[:, r0:r0 + STRIDE * (HROWS - 1) + 1:STRIDE, kw % STRIDE, kw // STRIDE:kw // STRIDE + WO]

                acc = CV[:, 0:HL].rearrange("p (r w) -> p r w", w=WO)
                mm(acc, wch[:, tap, :], window(xh), start=(tap == 0), stop=False)
                mm(acc, wcl[:, tap, :], window(xh), start=False, stop=False)
                last = mm(acc, wch[:, tap, :], window(xl), start=False, stop=(tap == TAPS - 1))
                if tap == TAPS - 1:
                    last.then_inc(conv_full, 1)

            taps = []

            def fill(l, place, n=None):
                floor = TAPS if l == 0 else 0
                for _ in range(max(0, min(FILL[l][place] if n is None else n, len(taps) - floor))):
                    conv_tap(*taps.pop(0))

            def layernorm(i, l, src):
                project(i, f"mean{l}", K["mean_w"][:], src)
                fill(l, "mean")
                pe.wait_ge(sq_ready, i * 3 + (l + 1))
                project(i, f"var{l}", K["mean_w"][:], sq[:])
                fill(l, "var")

            def values(i, a):
                use = f"v{a}"
                pe.wait_ge(t_read[slot(use)], before(i, use))
                for b in range(NB):
                    last = mm(T[slot(use)][0:KB, b // 3, (b % 3) * C:(b % 3 + 1) * C],
                              nx[:, b * KB:(b + 1) * KB], K[f"v{a}"][:])
                last.then_inc(t_full[slot(use)], 1)

            def scores_of(i, a, h, qb, hf, dst):
                return mm(dst[0:KB, hf, 0:HL], stack[0:MAXROW, 0, h, qb * KB:(qb + 1) * KB],
                          stack[0:MAXROW, 1, h, hf * HL:(hf + 1) * HL])

            def head_stacked(i, a, h):
                if a == 0 and h == 0:
                    pe.wait_ge(ones_ready, (i + 1) * 2)
                pe.wait_ge(stacked[h], i * ATT * STACK_IN + (a + 1) * STACK_IN)

            def max_pair(i, a, n):
                h, qb = divmod(n, NB)
                if qb == 0:
                    head_stacked(i, a, h)
                use = f"max{a}.{n}"
                pe.wait_ge(t_read[slot(use)], before(i, use))
                for hf in range(2):
                    last = scores_of(i, a, h, qb, hf, T[slot(use)])
                last.then_inc(t_full[slot(use)], 1)

            def max_tile(i, a, n):
                h, qb, hf = GH + n // (2 * NB), n // 2 % NB, n % 2
                if n % (2 * NB) == 0:
                    head_stacked(i, a, h)
                if a == 0 and n < 2:
                    pe.wait_ge(acc_read, i * E)
                pe.wait_ge(m_read[hf], (i * ATT + a) * TILES // 2 + n // 2)
                scores_of(i, a, h, qb, hf, M).then_inc(m_full[hf], 1)

            def max_rows(i, a, g):
                use = f"rows{a}{g}"
                pe.wait_ge(t_read[slot(use)], before(i, use))
                if g == 0:
                    for n in range(GROWS - 2, GROWS):
                        pe.wait_ge(t_read[slot(f"max{a}.{n}")], filled(i, f"max{a}.{n}"))
                else:
                    pe.wait_ge(rowmax_ready, i * ATT + (a + 1))
                nc.tensor.transpose(T[slot(use)][0:GROWS, 0, 0:KB], rm[:, g * GROWS:(g + 1) * GROWS],
                                    K["ident"][0:KB, 0:KB]).then_inc(t_full[slot(use)], 1)

            def scores(i, a, g, s, pair):
                qh, kb = divmod(s, NB)
                if s == 0 and pair == 0:
                    pe.wait_ge(rowmax_in, i * ATT * NG * 48 + (a * NG + g + 1) * 48)
                use = f"s{a}{g}.{s}.{pair}"
                pe.wait_ge(t_read[slot(use)], before(i, use))
                for j in range(2):
                    h = GH * g + 2 * pair + j
                    last = mm(T[slot(use)][0:KB, j, 0:HL], stack[:, 1, h, kb * KB:(kb + 1) * KB],
                              stack[:, 0, h, qh * HL:(qh + 1) * HL])
                last.then_inc(t_full[slot(use)], 1)

            def weighted(i, a, g, s):
                qh, kb = divmod(s, NB)
                if kb == 0:
                    pe.wait_ge(o_read, i * OUTS + ((a * NG + g) * 2 + qh))
                for pair in range(2):
                    use = f"s{a}{g}.{s}.{pair}"
                    pe.wait_ge(t_read[slot(use)], filled(i, use))
                for j in range(GH):
                    last = mm(O[32 * j:32 * (j + 1), 0:HL], V[:, kb, GH * g + j, :],
                              P[pair_no(a, g, s, j // 2) % NP][:, j % 2, :], start=(kb == 0), stop=(kb == NB - 1),
                              tile_position=(0, 32 * j))
                    if j % 2:
                        last.then_inc(pv_done, 1)

            def attention(i, a):
                fill(a, "split")
                for n in range(GROWS):
                    max_pair(i, a, n)
                    if n % 2 and n // 2 < FILL[a]["tiles"]:
                        fill(a, "tiles", 1)
                for n in range(2):
                    max_tile(i, a, n)
                max_rows(i, a, 0)
                for n in range(2, AHEAD):
                    fill(a, "rows0", 1)
                    max_tile(i, a, n)
                fill(a, "rows0", FILL[a]["rows0"] - (AHEAD - 2))
                n = AHEAD
                for s in range(STEPS):
                    for part in range(PER_STEP):
                        if part < 2:
                            scores(i, a, 0, s, part)
                        elif part == 2 and s:
                            weighted(i, a, 0, s - 1)
                        if n < TILES:
                            max_tile(i, a, n)
                            n += 1
                    if s == ROWS1_STEP:
                        max_rows(i, a, 1)
                weighted(i, a, 0, STEPS - 1)
                fill(a, "rows1")
                for s in range(STEPS):
                    for pair in range(2):
                        scores(i, a, 1, s, pair)
                    if s:
                        weighted(i, a, 1, s - 1)
                weighted(i, a, 1, STEPS - 1)
                if a == 1:
                    fill(a, "out")
                use = f"out{a}"
                pe.wait_ge(t_read[slot(use)], before(i, use))
                pe.wait_ge(on_ready, i * OUTS + (a + 1) * NG * 2)
                for hf in range(2):
                    for g in range(NG):
                        last = mm(T[slot(use)][:, hf, 0:HL], K[f"o{a}"][:, g, :], on[g][:, hf * HL:(hf + 1) * HL],
                                  start=(g == 0), stop=(g == NG - 1))
                last.then_inc(t_full[slot(use)], 1)

            def down(i, n):
                e, f = divmod(n, FB)
                if f == 0:
                    pe.wait_ge(acc_read, i * E + e)
                    if e == 0:
                        for s in range(2):
                            pe.wait_ge(m_read[s], (i + 1) * ATT * TILES // 2)
                use = f"h{e}.{f}"
                pe.wait_ge(t_read[slot(use)], filled(i, use))
                for hf in range(2):
                    last = mm(M[:, hf, 0:HL], K["w2"][:, n, :], hid[n % 3][:, hf * HL:(hf + 1) * HL],
                              start=(f == 0), stop=(f == FB - 1))
                last.then_inc(down_done, 1)

            def gate_rows(i, use, src, step):
                pe.wait_ge(t_read[slot(use)], before(i, use))
                pe.wait_ge(gate_step, i * 8 + step)
                for b in range(NB):
                    last = nc.tensor.transpose(T[slot(use)][0:E, b // 3, (b % 3) * KB:(b % 3 + 1) * KB], src[:, b, :],
                                               K["ident"][0:KB, 0:KB])
                last.then_inc(t_full[slot(use)], 1)

            def experts(i):
                use = "gate"
                pe.wait_ge(tok_ready, i + 1)
                pe.wait_ge(t_read[slot(use)], before(i, use))
                for b in range(NB):
                    last = mm(T[slot(use)][0:KB, 0, b * E:(b + 1) * E], tok[:, b * KB:(b + 1) * KB], K["gate_w"][:])
                last.then_inc(t_full[slot(use)], 1)
                for n in range(E * FB):
                    e, f = divmod(n, FB)
                    project(i, f"h{e}.{f}", K["w1"][:, n * C:(n + 1) * C], tok)
                    if n:
                        down(i, n - 1)
                    if n == 1:
                        gate_rows(i, "onehot", gt[:, 4], 5)
                        gate_rows(i, "weight", gt[:, 5], 8)
                    if f == 2 and e + 1 < E:
                        use = f"mask{e + 1}"
                        pe.wait_ge(t_read[slot(use)], before(i, use))
                        pe.wait_ge(t_read[slot("onehot")], filled(i, "onehot"))
                        for hf in range(2):
                            last = mm(T[slot(use)][:, hf, 0:HL], selb[:, e + 1, :], onehotT[:, hf * HL:(hf + 1) * HL])
                        last.then_inc(t_full[slot(use)], 1)
                down(i, E * FB - 1)
                pe.wait_ge(t_read[slot("weight")], filled(i, "weight"))
                project(i, "gw", K["ones8"][:], weightT)
                project(i, "b2", K["b2"][:], weightT)

            def body(i, next_conv, load_ahead):
                taps[:] = [(i + 1, half, tap) for half in range(2) for tap in range(TAPS)] if next_conv else []
                pe.wait_ge(conv_read, i * 2 + 2)
                layernorm(i, 0, hc)
                pe.wait_ge(n_ready, i * 3 + 1)
                for use in ("q0", "qp0", "k0", "kp0"):
                    project(i, use, K[use][:], nx)
                values(i, 0)
                attention(i, 0)
                pe.wait_ge(t_read[slot("out0")], filled(i, "out0"))
                layernorm(i, 1, h1)
                pe.wait_ge(n_ready, i * 3 + 2)
                for use in ("q1", "k1"):
                    project(i, use, K[use][:], nx)
                values(i, 1)
                attention(i, 1)
                pe.wait_ge(t_read[slot("out1")], filled(i, "out1"))
                layernorm(i, 2, xc)
                experts(i)

            pe.wait_ge(weights_split, 3)
            pe.wait_ge(consts_loaded, ALL_CONSTS)
            for half in range(2):
                for tap in range(TAPS):
                    conv_tap(0, half, tap)
            every_image(pe, body)

        @block.scalar
        def _(act):
            def evac_conv(m, half):
                act.wait_ge(conv_full, m * 2 + (half + 1))
                nc.scalar.activation(hc[:, half * HL:(half + 1) * HL], CV[:, 0:HL], ACT.Identity,
                                     bias=vec("conv_b")).then_inc(conv_read, 1)

            def layernorm(i, l):
                act.wait_ge(t_read[slot(f"mean{l}")], filled(i, f"mean{l}"))
                nc.scalar.activation(sq[:], xc[:], ACT.Square).then_inc(sq_ready, 1)
                use = f"var{l}"
                act.wait_ge(t_full[slot(use)], filled(i, use))
                nc.scalar.activation(halves(sq[:]), tv(use), ACT.Ln, bias=vec("eps")).then_inc(t_read[slot(use)], 1)
                act.wait_ge(t_read[slot(use)], filled(i, use))
                nc.scalar.activation(sq[:], sq[:], ACT.Exp, scale=-0.5).then_inc(rstd_ready, 1)

            def split(i, a):
                for z, name in enumerate(("q", "k")):
                    if a == 0:
                        act.wait_ge(rope_ready, i * 2 + (z + 1))
                    else:
                        use = f"{name}1"
                        act.wait_ge(t_full[slot(use)], filled(i, use))
                        nc.scalar.activation(halves(qk[:, z, :]), tv(use), ACT.Identity,
                                             bias=vec(use)).then_inc(t_read[slot(use)], 1)
                        act.wait_ge(t_read[slot(use)], filled(i, use))
                    nc.scalar.activation(parts[:, 3 * z, :], qk[:, z, :], ACT.Copy).then_inc(high_ready, 1)
                for z in range(2):
                    act.wait_ge(rest_ready, i * 2 * ATT + (2 * a + z + 1))
                    nc.scalar.activation(parts[:, 3 * z + 1, :], qk[:, z, :], ACT.Copy).then_inc(mid_ready, 1)

            def rows(i, a, g):
                use = f"rows{a}{g}"
                act.wait_ge(t_full[slot(use)], filled(i, use))
                nc.scalar.activation(rmt[:], T[slot(use)][0:GROWS, 0, 0:KB], ACT.Copy,
                                     scale=-1.0).then_inc(t_read[slot(use)], 1)

            def rows_in(i, a, g):
                act.wait_ge(ones_ready, (i + 1) * 2)
                act.wait_ge(rowmax_part, i * 20 + (a * NG + g + 1) * 5)
                for part in range(3):
                    dst = stack[MAXROW + part:MAXROW + part + 1, 0, GH * g:GH * (g + 1), :]
                    act.dma_start(dst.rearrange("p h n -> p (h n)").rearrange("p (c q) -> p c q", q=KB), rmp[:, part, :]).then_inc(rowmax_in, 16)

            def exps(i, a, g, s):
                if g == 0 and s == 0:
                    for h in range(H):
                        act.wait_ge(stacked[h], i * ATT * STACK_IN + (a + 1) * STACK_IN)
                for pair in range(2):
                    n, use = pair_no(a, g, s, pair), f"s{a}{g}.{s}.{pair}"
                    act.wait_ge(pv_done, i * PAIRS + max(n - (NP - 1), 0))
                    act.wait_ge(t_full[slot(use)], filled(i, use))
                    nc.scalar.activation(P[n % NP][:, :, :], T[slot(use)][0:KB, :, 0:HL], ACT.Exp,
                                         scale=SCALE).then_inc(t_read[slot(use)], 1)

            def evac_out(i, k):
                act.wait_ge(pv_done, i * PAIRS + (k + 1) * 2 * NB)
                act.wait_ge(on_ready, i * OUTS + k)
                nc.scalar.activation(o_sb, O[:, 0:HL], ACT.Copy).then_inc(o_read, 1)

            def invert_sums(i, k):
                act.wait_ge(sums_ready, i * OUTS + (k + 1))
                nc.scalar.activation(sums, sums, ACT.Ln).then_inc(log_ready, 1)
                act.wait_ge(log_ready, i * OUTS + (k + 1))
                nc.scalar.activation(sums, sums, ACT.Exp, scale=-1.0).then_inc(inverse_ready, 1)

            def attention(i, a):
                split(i, a)
                for g in range(NG):
                    k = (a * NG + g) * 2
                    if g == 0:
                        rows(i, a, 0)
                    rows_in(i, a, g)
                    for s in range(STEPS):
                        exps(i, a, g, s)
                        if s == 1 and g:
                            invert_sums(i, k - 1)
                        if s == NB:
                            evac_out(i, k)
                        if s == NB + 2:
                            invert_sums(i, k)
                        if g == 0 and s == ROWS1_STEP:
                            rows(i, a, 1)
                    evac_out(i, k + 1)
                invert_sums(i, k + 1)

            def experts(i):
                act.wait_ge(n_ready, i * 3 + 3)
                nc.scalar.activation(tok, nx[:], ACT.Identity, bias=vec("ln_b"), scale=vec("ln_g")).then_inc(tok_ready, 1)
                act.wait_ge(gate_step, i * 8 + 2)
                nc.scalar.activation(gt[:, 2], gt[:, 1], ACT.Exp).then_inc(gate_exp, 1)
                for n in range(E * FB):
                    e, f = divmod(n, FB)
                    use = f"h{e}.{f}"
                    act.wait_ge(down_done, i * E * FB + max(n - 2, 0))
                    act.wait_ge(t_full[slot(use)], filled(i, use))
                    nc.scalar.activation(halves(hid[n % 3]), tv(use), ACT.Gelu_apprx_tanh,
                                         bias=K["b1"][:, n:n + 1]).then_inc(t_read[slot(use)], 1)
                    if n == 1:
                        for use, dst in (("onehot", onehotT), ("weight", weightT)):
                            act.wait_ge(t_full[slot(use)], filled(i, use))
                            nc.scalar.activation(halves(dst[:]), T[slot(use)][0:E, :, 0:HL],
                                                 ACT.Copy).then_inc(t_read[slot(use)], 1)
                    if f == 2 and e + 1 < E:
                        use = f"mask{e + 1}"
                        act.wait_ge(acc_read, i * E + e)
                        act.wait_ge(t_full[slot(use)], filled(i, use))
                        nc.scalar.activation(halves(mask[(e + 1) % 2]), tv(use), ACT.Copy).then_inc(t_read[slot(use)], 1)

            def body(i, next_conv, load_ahead):
                act.preload_act_table_set("natural_log_exp_and_others")
                layernorm(i, 0)
                attention(i, 0)
                act.wait_ge(t_read[slot("out0")], filled(i, "out0"))
                if next_conv:
                    evac_conv(i + 1, 0)
                layernorm(i, 1)
                attention(i, 1)
                layernorm(i, 2)
                if next_conv:
                    evac_conv(i + 1, 1)
                experts(i)

            act.wait_ge(consts_loaded, ALL_CONSTS)
            for half in range(2):
                evac_conv(0, half)
            every_image(act, body)

        @block.vector
        def _(dve):
            def split_rows(m, half):
                dve.wait_ge(conv_full, m * 2 + half)
                for c in range(CH):
                    row0, rows = CHUNKS[half][c]
                    n = CH * half + c
                    b, r = n % 2, PAD + row0 - ROW0[half]
                    dve.wait_ge(raw_in[b], m * 16 * CH + 16 * (n // 2 + 1))
                    src = raw[b][:, 0:rows, :].rearrange("p r (w s) -> p r s w", s=STRIDE)
                    hi = xh[:, r:r + rows, :, 1:1 + WI // STRIDE]
                    lo = xl[:, r:r + rows, :, 1:1 + WI // STRIDE]
                    nc.vector.tensor_copy(hi, src).then_inc(x_high, 1)
                    dve.wait_ge(x_high, m * CPI + (n + 1))
                    nc.vector.tensor_tensor(lo, src, hi.bitcast(F32), ALU.subtract).then_inc(x_split, 1)

            def centre(i, l, src):
                use = f"mean{l}"
                dve.wait_ge(t_full[slot(use)], filled(i, use))
                nc.vector.tensor_tensor(halves(xc[:]), halves(src[:]), tv(use), ALU.subtract).then_inc(t_read[slot(use)], 1)

            def normalise(i, l):
                dve.wait_ge(rstd_ready, i * 3 + (l + 1))
                nc.vector.tensor_tensor(nx[:], xc[:], sq[:], ALU.mult).then_inc(n_ready, 1)

            def rope(i, z, name):
                for use, table, dst in ((f"{name}0", "cos", xc), (f"{name}p0", "sin", sq)):
                    dve.wait_ge(n_ready, i * 3 + 1) if z == 0 else dve.wait_ge(rope_ready, i * 2 + z)
                    dve.wait_ge(t_full[slot(use)], filled(i, use))
                    nc.vector.scalar_tensor_tensor(halves(dst[:]), tv(use), vec(use), halves(K[table][:]),
                                                   ALU.add, ALU.mult).then_inc(t_read[slot(use)], 1)
                for use in (f"{name}0", f"{name}p0"):
                    dve.wait_ge(t_read[slot(use)], filled(i, use))
                nc.vector.tensor_tensor(qk[:, z, :], xc[:], sq[:], ALU.add).then_inc(rope_ready, 1)

            def rest(i, a, z):
                n = i * 2 * ATT + (2 * a + z + 1)
                dve.wait_ge(high_ready, n)
                nc.vector.tensor_tensor(qk[:, z, :], qk[:, z, :], parts[:, 3 * z, :], ALU.subtract).then_inc(rest_ready, 1)

            def low(i, a, z):
                n = i * 2 * ATT + (2 * a + z + 1)
                dve.wait_ge(mid_ready, n)
                nc.vector.tensor_tensor(parts[:, 3 * z + 2, :], qk[:, z, :], parts[:, 3 * z + 1, :],
                                        ALU.subtract).then_inc(low_ready, 1)

            def values(i, a):
                use = f"v{a}"
                dve.wait_ge(t_full[slot(use)], filled(i, use))
                for bank in range(2):
                    src = T[slot(use)][0:KB, bank, 0:3 * C]
                    for b in range(3):
                        last = nc.vector.tensor_tensor(
                            V[:, 3 * bank + b, :, 0:HD], src[:, b * C:(b + 1) * C].rearrange("p (h d) -> p h d", d=HD),
                            K[f"bv{a}"][:, :].rearrange("p (h d) -> p h d", d=HD), ALU.add)
                last.then_inc(t_read[slot(use)], 1)

            def reduce_pair(i, a, n):
                use = f"max{a}.{n}"
                dve.wait_ge(t_full[slot(use)], filled(i, use))
                nc.vector.tensor_reduce(rm[:, n:n + 1], T[slot(use)][0:KB, :, 0:HL], AX.XY,
                                        ALU.max).then_inc(t_read[slot(use)], 1)

            def reduce_tile(i, a, n):
                hf = n % 2
                dve.wait_ge(m_full[hf], (i * ATT + a) * TILES // 2 + (n // 2 + 1))
                nc.vector.tensor_reduce(rm2[:, n // 2, hf:hf + 1], M[0:KB, hf, 0:HL], AX.X, ALU.max).then_inc(m_read[hf], 1)

            def join_halves(i, a):
                for hf in range(2):
                    dve.wait_ge(m_read[hf], (i * ATT + (a + 1)) * TILES // 2)
                nc.vector.tensor_reduce(rm[:, GROWS:2 * GROWS], rm2[:], AX.X, ALU.max).then_inc(rowmax_ready, 1)

            def row_max_parts(i, a, g):
                use = f"rows{a}{g}"
                step = i * 20 + (a * NG + g) * 5
                dve.wait_ge(t_read[slot(use)], filled(i, use))
                for part in range(3):
                    nc.vector.tensor_copy(rmp[:, part, :], rmt[:]).then_inc(rowmax_part, 1)
                    if part < 2:
                        dve.wait_ge(rowmax_part, step + (2 * part + 1))
                        nc.vector.tensor_tensor(rmt[:], rmt[:], rmp[:, part, :], ALU.subtract).then_inc(rowmax_part, 1)
                        dve.wait_ge(rowmax_part, step + (2 * part + 2))

            def spread_sums(i, k):
                dve.wait_ge(o_read, i * OUTS + (k + 1))
                hold(dve)
                nc.vector.stream_shuffle(sums, o_sb, [HD + r % HD for r in range(32)]).then_inc(sums_ready, 1)

            def attention(i, a, next_conv):
                k = a * NG * 2
                for n in range(GROWS):
                    reduce_pair(i, a, n)
                for n in range(2):
                    reduce_tile(i, a, n)
                row_max_parts(i, a, 0)
                for n in range(2, AHEAD):
                    reduce_tile(i, a, n)
                n = AHEAD
                for s in range(STEPS):
                    for _ in range(PER_STEP):
                        if n < TILES:
                            reduce_tile(i, a, n)
                            n += 1
                            if n == TILES:
                                join_halves(i, a)
                    if s == NB + 1:
                        spread_sums(i, k)
                row_max_parts(i, a, 1)
                spread_sums(i, k + 1)
                if a == 0 and next_conv:
                    split_rows(i + 1, 1)
                spread_sums(i, k + 2)
                spread_sums(i, k + 3)

            def add_out(i, a, dst, residual):
                use = f"out{a}"
                dve.wait_ge(t_full[slot(use)], filled(i, use))
                nc.vector.scalar_tensor_tensor(halves(dst[:]), tv(use), vec(f"o{a}"), halves(residual[:]),
                                               ALU.add, ALU.add).then_inc(t_read[slot(use)], 1)
                dve.wait_ge(t_read[slot(use)], filled(i, use))

            def gate(i):
                def per_token(ap):
                    return ap.unsqueeze(2).to_broadcast([KB, NB, E])

                base = i * 8
                dve.wait_ge(t_full[slot("gate")], filled(i, "gate"))
                nc.vector.tensor_tensor(gt[:, 0], T[slot("gate")][0:KB, 0, 0:NB * E].rearrange("p (b e) -> p b e", e=E),
                                        K["gate_b"][:], ALU.add).then_inc(t_read[slot("gate")], 1)
                dve.wait_ge(t_read[slot("gate")], filled(i, "gate"))
                nc.vector.tensor_reduce(gs[:, 0], gt[:, 0], AX.X, ALU.max).then_inc(gate_step, 1)
                dve.wait_ge(gate_step, base + 1)
                nc.vector.tensor_tensor(gt[:, 1], gt[:, 0], per_token(gs[:, 0]), ALU.subtract).then_inc(gate_step, 1)
                dve.wait_ge(gate_step, base + 2)
                nc.vector.scalar_tensor_tensor(gt[:, 3], gt[:, 1], 0.0, K["key"][:], ALU.is_ge, ALU.mult).then_inc(gate_step, 1)
                dve.wait_ge(gate_step, base + 3)
                nc.vector.tensor_reduce(gs[:, 1], gt[:, 3], AX.X, ALU.max).then_inc(gate_step, 1)
                dve.wait_ge(gate_step, base + 4)
                nc.vector.tensor_tensor(gt[:, 4], gt[:, 3], per_token(gs[:, 1]), ALU.is_equal).then_inc(gate_step, 1)
                dve.wait_ge(gate_exp, i + 1)
                nc.vector.tensor_reduce(gs[:, 2], gt[:, 2], AX.X, ALU.add).then_inc(gate_step, 1)
                dve.wait_ge(gate_step, base + 6)
                nc.vector.reciprocal(gs[:, 3], gs[:, 2]).then_inc(gate_step, 1)
                dve.wait_ge(gate_step, base + 7)
                nc.vector.tensor_tensor(gt[:, 5], gt[:, 4], per_token(gs[:, 3]), ALU.mult).then_inc(gate_step, 1)

            def take_expert(i, e):
                dve.wait_ge(down_done, i * E * FB + (e + 1) * FB)
                if e == 0:
                    dve.wait_ge(stored, i * 16)
                    nc.vector.tensor_copy(halves(sel), M[:, :, 0:HL]).then_inc(acc_read, 1)
                else:
                    use = f"mask{e}"
                    dve.wait_ge(t_read[slot(use)], filled(i, use))
                    dve.wait_ge(acc_read, i * E + e)
                    hold(dve)
                    nc.vector.copy_predicated(halves(sel), halves(mask[e % 2].bitcast(U16)),
                                              M[:, :, 0:HL]).then_inc(acc_read, 1)

            def finish(i):
                dve.wait_ge(acc_read, (i + 1) * E)
                for use, op in (("gw", ALU.mult), ("b2", ALU.add)):
                    dve.wait_ge(t_full[slot(use)], filled(i, use))
                    nc.vector.tensor_tensor(halves(sel), halves(sel), tv(use), op).then_inc(t_read[slot(use)], 1)
                    dve.wait_ge(t_read[slot(use)], filled(i, use))
                nc.vector.tensor_tensor(sel, sel, h1[:], ALU.add).then_inc(y_ready, 1)

            def body(i, next_conv, load_ahead):
                centre(i, 0, hc)
                normalise(i, 0)
                rope(i, 0, "q")
                rope(i, 1, "k")
                rest(i, 0, 0)
                values(i, 0)
                rest(i, 0, 1)
                low(i, 0, 0)
                low(i, 0, 1)
                attention(i, 0, next_conv)
                add_out(i, 0, h1, hc)
                centre(i, 1, h1)
                normalise(i, 1)
                rest(i, 1, 0)
                rest(i, 1, 1)
                values(i, 1)
                low(i, 1, 0)
                low(i, 1, 1)
                attention(i, 1, next_conv)
                add_out(i, 1, xc, nx)
                centre(i, 2, xc)
                normalise(i, 2)
                gate(i)
                if load_ahead:
                    split_rows(i + 2, 0)
                for e in range(E):
                    take_expert(i, e)
                finish(i)

            dve.wait_ge(cleared, 3)
            split_rows(0, 0)
            dve.wait_ge(conv_w_loaded, 32)
            staged = ((slice(0, BIG_TAPS), bigf[:, 0:BIG_TAPS * C]),
                      (slice(BIG_TAPS, TAPS), qk[:, :, :].rearrange("p a b -> p (a b)")[:, 0:(TAPS - BIG_TAPS) * C]))
            for n, (t, src) in enumerate(staged):
                w = src.rearrange("p (t n) -> p t n", n=C)
                nc.vector.tensor_copy(wch[:, t, :], w)
            dve.wait_ge(consts_loaded, ALL_CONSTS)
            nc.vector.tensor_copy(selb[:], parts[:, :, :].rearrange("p a b -> p (a b)").bitcast(F32)[0:E, 0:E * C].rearrange(
                "p (e n) -> p e n", n=C)).then_inc(weights_split, 1)
            dve.wait_ge(weights_split, 1)
            for n, (t, src) in enumerate(staged):
                w = src.rearrange("p (t n) -> p t n", n=C)
                nc.vector.tensor_tensor(wcl[:, t, :], w, wch[:, t, :].bitcast(F32), ALU.subtract).then_inc(weights_split, 1)
            split_rows(0, 1)
            split_rows(1, 0)
            every_image(dve, body)

        @block.gpsimd
        def _(pool):
            nc.gpsimd.memset(xh[:, :, :, :].bitcast(F32), 0.0).then_inc(cleared, 1)
            nc.gpsimd.memset(xl[:, :, :, :].bitcast(F32), 0.0).then_inc(cleared, 1)
            nc.gpsimd.memset(V[:], 1.0).then_inc(cleared, 1)

            def body(i, next_conv, load_ahead):
                pool.wait_ge(weights_split, 3)
                pool.wait_ge(stored, i * 16)
                pool.wait_ge(n_ready, i * 3 + 1)
                hold(pool)
                nc.gpsimd.memset(stack[SROWS:C, 0, :, :], 0.0).then_inc(ones_ready, 1)
                nc.gpsimd.memset(stack[SROWS:C, 1, :, :], 1.0).then_inc(ones_ready, 1)
                for k in range(OUTS):
                    g, qh = k // 2 % NG, k % 2
                    pool.wait_ge(inverse_ready, i * OUTS + (k + 1))
                    nc.gpsimd.tensor_tensor(on[g][:, qh * HL:(qh + 1) * HL], o_sb, sums, ALU.mult).then_inc(on_ready, 1)

            every_image(pool, body)


def layouts(p):
    n = np.arange(C)
    turned = np.where(n % 8 < 4, n + 4, n - 4)
    sign = np.where(n % 8 < 4, -1.0, 1.0).astype(np.float32)
    freq = (1.0 / np.float32(10000.0) ** (np.arange(0, HD, 2, dtype=np.float32) / np.float32(HD))).astype(np.float32)
    angle = freq[n % 8][:, None] * np.arange(L, dtype=np.float32)[None, :]

    def heads(w):
        r = np.zeros((C, NG, C), np.float32)
        for h in range(H):
            r[32 * (h % GH):32 * (h % GH) + HD, h // GH, :] = w[HD * h:HD * (h + 1), :]
        return r

    def rows(v):
        return np.broadcast_to(v, (KB, C))

    qkv, qkv_b = p["L0_attn_qkv_w"], p["L0_attn_qkv_b"]
    wq, wk, wv = (qkv[C * j:C * (j + 1)].T for j in range(3))
    bq, bk, bv = (qkv_b[C * j:C * (j + 1)] for j in range(3))
    vecs = [p["L0_tok_b"], bq, bq[turned], bk, bk[turned], p["L0_ffn_bq"], p["L0_ffn_bk"], p["L0_attn_out_b"],
            p["L0_ffn_bo"], p["L0_ffn_ln1_g"], p["L0_ffn_ln1_b"], np.full(C, EPS, np.float32)]
    consts = {
        "mean_w": np.full((C, C), 1.0 / C, np.float32), "ident": np.eye(C, dtype=np.float32),
        "cos": np.cos(angle).astype(np.float32), "sin": (np.sin(angle) * sign[:, None]).astype(np.float32),
        "key": np.broadcast_to(np.arange(E, 0, -1, dtype=np.float32), (KB, NB, E)),
        "ones8": np.ones((E, C), np.float32), "vecs": np.stack(vecs, 1),
        "b1": p["L0_ffn_b1"].reshape(E * FB, C).T,
        "q0": wq, "qp0": wq[:, turned], "k0": wk, "kp0": wk[:, turned], "v0": wv,
        "q1": p["L0_ffn_Wq"], "k1": p["L0_ffn_Wk"], "v1": p["L0_ffn_Wv"],
        "bv0": rows(bv), "bv1": rows(p["L0_ffn_bv"]),
        "o0": heads(p["L0_attn_out_w"].T), "o1": heads(p["L0_ffn_Wo"]),
        "gate_w": p["L0_ffn_gate_W"], "gate_b": np.broadcast_to(p["L0_ffn_gate_b"], (KB, NB, E)),
        "w1": p["L0_ffn_W1"].transpose(1, 0, 2).reshape(C, E * FF),
        "w2": p["L0_ffn_W2"].reshape(E * FB, C, C).transpose(1, 0, 2), "b2": p["L0_ffn_b2"],
    }
    w_conv = p["L0_tok_W"].reshape(C, C, TAPS).transpose(1, 2, 0)
    sel_rows = np.repeat(np.eye(E, dtype=np.float32), C, axis=1)
    return w_conv, sel_rows, consts


def kernel(**inputs):
    import concourse.bacc as _bacc
    from concourse.bass_utils import run_bass_kernel_spmd as _run

    p = {k: np.asarray(v) for k, v in inputs.items()}
    w_conv, sel_rows, consts = layouts(p)
    arrays = {"x": p["x"], "w_conv": w_conv, "sel_rows": sel_rows, **{f"c_{k}": v for k, v in consts.items()}}
    arrays = {k: np.ascontiguousarray(v) for k, v in arrays.items()}
    nc = _bacc.Bacc("TRN2", target_bir_lowering=False, num_devices=1)
    ap = {k: nc.dram_tensor(k, v.shape, mybir.dt.from_np(v.dtype), kind="ExternalInput").ap() for k, v in arrays.items()}
    out = nc.dram_tensor("out", (B, C, L), F32, kind="ExternalOutput").ap()
    build(nc, ap["x"], ap["w_conv"], ap["sel_rows"], {k: ap[f"c_{k}"] for k in LOADS}, out)
    r = _run(nc, [arrays], core_ids=[0])
    return np.ascontiguousarray(r.results[0]["out"].transpose(0, 2, 1))
```

```python
from contextlib import ExitStack

import numpy as np

import concourse.bass as bass
from concourse import mybir

F32 = mybir.dt.float32
F32R = mybir.dt.float32r
BF16 = mybir.dt.bfloat16
U16 = mybir.dt.uint16
ALU = mybir.AluOpType
ACT = mybir.ActivationFunctionType
AX = mybir.AxisListType

B, C, HI, WI = 16, 128, 60, 108
KH, STRIDE, PAD = 7, 3, 3
HO, WO = (HI + 2 * PAD - KH) // STRIDE + 1, (WI + 2 * PAD - KH) // STRIDE + 1
TAPS = KH * KH
L = HO * WO
HL = L // 2
H, HD = 8, C // 8
KB = 120
NB = L // KB
GH = 4
NG = H // GH
ATT = 2
STEPS = 2 * NB
GROWS = GH * NB
TILES = 2 * GROWS
SP_HEADS = 6
EARLY_HEADS = 2
ONES_FROM = (0, EARLY_HEADS, SP_HEADS)
ONES = 2 * len(ONES_FROM)
AHEAD = 8
PER_STEP = 5
ROWS1_STEP = 10
PAIRS = ATT * NG * STEPS * 2
NP = 4
OUTS = ATT * NG * 2
E, FF = 8, 4 * C
FB = FF // C
EPS = 1e-5
SCALE = 1.0 / float(HD) ** 0.5

HROWS = HO // 2
XROWS = 37
XCOLS = (WI + 2 * PAD) // STRIDE
ROW0 = (0, 27)
BASE = (0, PAD)
CHUNKS = (((0, 11), (11, 10), (21, 10)), ((27, 11), (38, 11), (49, 11)))
CH = 3
CPI = 2 * CH
RAW_ROWS = 11
BIG_TAPS = 40

TERMS = ((0, 0), (0, 1), (1, 0), (1, 1), (0, 2), (2, 0))
SROWS = HD * len(TERMS)
MAXROW = C - 3
STACK_IN = 16 * len(TERMS)


def slot_uses():
    u = []
    for a in range(ATT):
        u += ["mean1", "var1", "q1", "k1", "v1"] if a == 1 else []
        u += [f"max{a}.{n}" for n in range(GROWS)] + [f"rows{a}0"]
        for g in range(NG):
            for s in range(STEPS):
                u += [f"s{a}{g}.{s}.{pair}" for pair in range(2)]
                if (g, s) == (0, ROWS1_STEP):
                    u += [f"rows{a}1"]
        u += [f"out{a}"]
    u += ["mean2", "var2"]
    for e in range(E):
        for f in range(FB):
            u += [f"h{e}.{f}"]
            if (e, f) == (0, 1):
                u += ["onehot", "weight"]
            if f == 2 and e + 1 < E:
                u += [f"mask{e + 1}"]
    return u + ["gw", "b2"]


T_INDEX = {name: n for n, name in enumerate(slot_uses())}
assert len(T_INDEX) % 2 == 0
T_PER = len(T_INDEX) // 2


def slot(use):
    return T_INDEX[use] % 2


def filled(i, use):
    return i * T_PER + (T_INDEX[use] // 2 + 1)


def before(i, use):
    return i * T_PER + T_INDEX[use] // 2


def pair_no(a, g, s, pair):
    return ((a * NG + g) * STEPS + s) * 2 + pair


LOADS = {
    "mean_w": [C, C], "ident": [C, C], "cos": [C, L], "sin": [C, L], "key": [KB, NB, E], "ones8": [E, C],
    "vecs": [C, 12], "b1": [C, E * FB], "q0": [C, C], "qp0": [C, C], "k0": [C, C], "kp0": [C, C], "v0": [C, C],
    "q1": [C, C], "k1": [C, C], "v1": [C, C], "bv0": [KB, C], "bv1": [KB, C],
    "o0": [C, NG, C], "o1": [C, NG, C], "gate_w": [C, E], "gate_b": [KB, NB, E],
    "w1": [C, E * FF], "w2": [C, E * FB, C], "b2": [E, C],
}
VEC = {n: k for k, n in enumerate(
    ["conv_b", "q0", "qp0", "k0", "kp0", "q1", "k1", "o0", "o1", "ln_g", "ln_b", "eps"])}

FILL = ({"split": 0, "tiles": 33, "rows0": 7, "rows1": TAPS},
        {"mean": 3, "var": 4, "split": 20, "tiles": 8, "rows0": 7, "rows1": TAPS})

PIECES = [(name, hf) for z in "qk" for hf in range(2) for name in (f"{z}0", f"{z}p0")] + [("v0", 0), ("v0", 1)]
EARLY = 3
HIGH_AT, MIDDLE_AT = 11, 15


def build(nc, x, w_conv, sel_rows, consts, out):
    with ExitStack() as ctx:
        def sb(name, shape, dt=F32):
            return ctx.enter_context(nc.sbuf_tensor(name, shape, dt))

        def psum(name, shape):
            return ctx.enter_context(nc.psum_tensor(name, shape, F32))

        def sem(name):
            return ctx.enter_context(nc.semaphore(name))

        T = [psum(f"T{s}", [128, 2, 512]) for s in range(2)]
        M = psum("M", [128, 2, 512])
        O = psum("O", [128, 512])
        CV = psum("CV", [128, 512])

        def halves(ap):
            return ap.rearrange("p (a b) -> p a b", a=2)

        def tv(use):
            return T[slot(use)][:, :, 0:HL]

        wch, wcl = sb("wch", [C, TAPS, C], F32R), sb("wcl", [C, TAPS, C], F32R)
        K = {name: sb(name, shape) for name, shape in LOADS.items()}
        selb = sb("selb", [E, E, C], BF16)

        def vec(name):
            return K["vecs"][:, VEC[name]:VEC[name] + 1]

        raw = [sb(f"raw{n}", [C, RAW_ROWS, WI]) for n in range(2)]
        xh = sb("xh", [C, XROWS, STRIDE, XCOLS], F32R)
        xl = sb("xl", [C, XROWS, STRIDE, XCOLS], F32R)
        hc, h1, nx = sb("hc", [C, L]), sb("h1", [C, L]), sb("nx", [C, L])
        xc, sq = sb("xc", [C, L]), sb("sq", [C, L])
        qk = sb("qk", [C, 2, L])
        parts = sb("parts", [C, 6, L], BF16)
        V = sb("V", [KB, NB, H, 32])
        rm2, rm = sb("rm2", [KB, GROWS, 2]), sb("rm", [KB, NG * GROWS])
        rmt, rmp = sb("rmt", [GROWS, KB]), sb("rmp", [GROWS, 3, KB], BF16)
        gt, gs = sb("gt", [KB, 6, NB, E]), sb("gs", [KB, 4, NB])
        onehotT, weightT = sb("onehotT", [E, L], BF16), sb("weightT", [E, L])
        P = [parts[:, 2 * n:2 * n + 2, :].rearrange("p a b -> p (a b)").bitcast(F32)[0:KB, :].rearrange(
            "p (j q) -> p j q", j=2) for n in range(3)] + [sq[0:KB, :].rearrange("p (j q) -> p j q", j=2)]
        xc0, sq0, nx0 = (parts[:, 2 * n:2 * n + 2, :].rearrange("p a b -> p (a b)").bitcast(F32) for n in range(3))
        big = sb("big", [128, H * 2 * L], BF16)
        stack = big[:, :].rearrange("p (s h n) -> p s h n", h=H, s=2)
        bigf = big[:, :].bitcast(F32)
        tok = bigf[:, L:2 * L]
        hid = [bigf[:, n * L:(n + 1) * L] for n in (2, 3, 5)]
        mask = [big[:, (12 + n) * L:(13 + n) * L] for n in range(2)]
        sel = bigf[:, 7 * L:8 * L]
        o_sb, sums = xc[:, 0:HL], xc[:, HL:L]
        on = [qk[:, g, :] for g in range(NG)]

        conv_w_loaded, consts_loaded = sem("conv_w_loaded"), sem("consts_loaded")
        weights_split, cleared = sem("weights_split"), sem("cleared")
        t_full, t_read = [sem(f"t_full{s}") for s in range(2)], [sem(f"t_read{s}") for s in range(2)]
        m_full, m_read = [sem(f"m_full{s}") for s in range(2)], [sem(f"m_read{s}") for s in range(2)]
        o_read = sem("o_read")
        conv_full, conv_read = sem("conv_full"), sem("conv_read")
        raw_in = [sem(f"raw_in{n}") for n in range(2)]
        x_high, x_split = sem("x_high"), sem("x_split")
        sq_ready, log_ready, rstd_ready, n_ready = sem("sq_ready"), sem("log_ready"), sem("rstd_ready"), sem("n_ready")
        stats_full, stats_read = sem("stats_full"), sem("stats_read")
        sq0_ready, rstd0_ready, n0_ready = sem("sq0_ready"), sem("rstd0_ready"), sem("n0_ready")
        piece_full, piece_read = sem("piece_full"), sem("piece_read")
        rope_ready = sem("rope_ready")
        high_ready, rest_ready, mid_ready, low_ready = (sem(f"{n}_ready") for n in ("high", "rest", "mid", "low"))
        ones_ready = sem("ones_ready")
        stacked = [sem(f"stacked{h}") for h in range(H)]
        rowmax_ready, rowmax_part, rowmax_in = sem("rowmax_ready"), sem("rowmax_part"), sem("rowmax_in")
        pv_done = sem("pv_done")
        sums_ready, inverse_ready, on_ready = sem("sums_ready"), sem("inverse_ready"), sem("on_ready")
        tok_ready = sem("tok_ready")
        gate_full, gate_read = sem("gate_full"), sem("gate_read")
        gate_step, gate_exp = sem("gate_step"), sem("gate_exp")
        down_done, acc_read = sem("down_done"), sem("acc_read")
        y_ready, stored = sem("y_ready"), sem("stored")

        held = {nc.vector.engine: sem("held_vector"), nc.gpsimd.engine: sem("held_gpsimd")}

        ALL_CONSTS = 16 * (len(LOADS) + 1)

        def hold(eng):
            eng.sem_inc(held[eng.engine], 1)

        def first(m):
            return isinstance(m, int) and m == 0

        def every_image(eng, body):
            body(0, True, True)
            with eng.Fori(1, B - 2) as i:
                body(i, True, True)
            body(B - 2, True, False)
            body(B - 1, False, False)

        def stack_heads(eng, i, a, heads):
            eng.wait_ge(low_ready, i * 2 * ATT + (2 * a + 2))
            if eng.engine in held:
                hold(eng)
            for h in heads:
                for r, (qp, kp) in enumerate(TERMS):
                    eng.dma_start(stack[HD * r:HD * (r + 1), :, h, :],
                                  parts[HD * h:HD * (h + 1), qp:4 + kp:3 + kp - qp, :]).then_inc(stacked[h], 16)

        block = ctx.enter_context(nc.Block())

        @block.sync
        def _(sp):
            def load_rows(m, half, chunks=range(CH)):
                for c in chunks:
                    row0, rows = CHUNKS[half][c]
                    n, b = CH * half + c, (CH * half + c) % 2
                    if not (isinstance(m, int) and CPI * m + n < 2):
                        sp.wait_ge(x_split, m * CPI + (n - 1))
                    sp.dma_start(raw[b][:, 0:rows, :], x[m, :, row0:row0 + rows, :]).then_inc(raw_in[b], 16)

            load_rows(0, 0)
            sp.dma_start(bigf[:, 0:BIG_TAPS * C].rearrange("p (t n) -> p t n", n=C),
                         w_conv[:, 0:BIG_TAPS, :]).then_inc(conv_w_loaded, 16)
            sp.dma_start(qk[:, :, :].rearrange("p a b -> p (a b)")[:, 0:(TAPS - BIG_TAPS) * C].rearrange(
                "p (t n) -> p t n", n=C), w_conv[:, BIG_TAPS:TAPS, :]).then_inc(conv_w_loaded, 16)
            for name in LOADS:
                sp.dma_start(K[name][:], consts[name]).then_inc(consts_loaded, 16)
            sp.dma_start(parts[:, :, :].rearrange("p a b -> p (a b)").bitcast(F32)[0:E, 0:E * C],
                         sel_rows).then_inc(consts_loaded, 16)
            load_rows(0, 1)
            load_rows(1, 0)

            def body(i, next_conv, load_ahead):
                sp.wait_ge(y_ready, i)
                stack_heads(sp, i, 0, range(EARLY_HEADS, SP_HEADS))
                if next_conv:
                    load_rows(i + 1, 1)
                if load_ahead:
                    load_rows(i + 2, 0, range(CH - 1))
                stack_heads(sp, i, 1, range(SP_HEADS))
                if load_ahead:
                    load_rows(i + 2, 0, [CH - 1])
                if next_conv:
                    stack_heads(sp, i + 1, 0, range(EARLY_HEADS))
                sp.wait_ge(y_ready, i + 1)
                sp.dma_start(out[i], sel).then_inc(stored, 16)

            stack_heads(sp, 0, 0, range(EARLY_HEADS))
            every_image(sp, body)
            sp.wait_ge(stored, B * 16)

        @block.tensor
        def _(pe):
            def mm(out_ap, lhsT, rhs, start=True, stop=True, **kw):
                return nc.tensor.matmul(out_ap, lhsT, rhs, start=start, stop=stop, skip_group_check=True, **kw)

            def project(i, use, w, src):
                pe.wait_ge(t_read[slot(use)], before(i, use))
                for hf in range(2):
                    last = mm(T[slot(use)][0:w.shape[-1], hf, 0:HL], w, src[:, hf * HL:(hf + 1) * HL])
                last.then_inc(t_full[slot(use)], 1)

            def conv_tap(m, half, tap):
                if tap == 0:
                    pe.wait_ge(x_split, m * CPI + CH * (half + 1))
                    pe.wait_ge(conv_read, m * 2 + half)
                kh, kw = divmod(tap, KH)
                r0 = BASE[half] + kh

                def window(t):
                    return t[:, r0:r0 + STRIDE * (HROWS - 1) + 1:STRIDE, kw % STRIDE, kw // STRIDE:kw // STRIDE + WO]

                acc = CV[:, 0:HL].rearrange("p (r w) -> p r w", w=WO)
                mm(acc, wch[:, tap, :], window(xh), start=(tap == 0), stop=False)
                mm(acc, wcl[:, tap, :], window(xh), start=False, stop=False)
                last = mm(acc, wch[:, tap, :], window(xl), start=False, stop=(tap == TAPS - 1))
                if tap == TAPS - 1:
                    last.then_inc(conv_full, 1)

            taps = []

            def fill(l, place, n=None):
                floor = TAPS if l == 0 else 0
                for _ in range(max(0, min(FILL[l][place] if n is None else n, len(taps) - floor))):
                    conv_tap(*taps.pop(0))

            def layernorm(i, l, src):
                project(i, f"mean{l}", K["mean_w"][:], src)
                if l == 1:
                    fill(l, "mean")
                pe.wait_ge(sq_ready, i * 2 + l)
                project(i, f"var{l}", K["mean_w"][:], sq[:])
                if l == 1:
                    fill(l, "var")

            def values(i):
                use = "v1"
                pe.wait_ge(t_read[slot(use)], before(i, use))
                for b in range(NB):
                    last = mm(T[slot(use)][0:KB, b // 3, (b % 3) * C:(b % 3 + 1) * C],
                              nx[:, b * KB:(b + 1) * KB], K["v1"][:])
                last.then_inc(t_full[slot(use)], 1)

            def first_mean(m):
                pe.wait_ge(conv_read, m * 2 + 2)
                for hf in range(2):
                    if not first(m):
                        pe.wait_ge(m_read[hf], m * ATT * TILES // 2)
                    last = mm(M[:, hf, 0:HL], K["mean_w"][:], hc[:, hf * HL:(hf + 1) * HL])
                last.then_inc(stats_full, 1)

            def first_variance(m):
                pe.wait_ge(sq0_ready, m + 1)
                for hf in range(2):
                    last = mm(M[:, hf, 0:HL], K["mean_w"][:], sq0[:, hf * HL:(hf + 1) * HL])
                last.then_inc(stats_full, 1)

            def piece(m, n):
                name, hf = PIECES[n]
                if n == 0:
                    pe.wait_ge(n0_ready, m + 1)
                    if not first(m):
                        pe.wait_ge(o_read, m * OUTS)
                pe.wait_ge(piece_read, m * len(PIECES) + n)
                if name == "v0":
                    for b in range(3):
                        t = (3 * hf + b) * KB
                        last = mm(O[0:KB, b * C:(b + 1) * C], nx0[:, t:t + KB], K["v0"][:])
                else:
                    last = mm(O[:, 0:HL], K[name][:], nx0[:, hf * HL:(hf + 1) * HL])
                last.then_inc(piece_full, 1)

            def scores_of(i, a, h, qb, hf, dst):
                return mm(dst[0:KB, hf, 0:HL], stack[0:MAXROW, 0, h, qb * KB:(qb + 1) * KB],
                          stack[0:MAXROW, 1, h, hf * HL:(hf + 1) * HL])

            def head_stacked(i, a, h):
                if a == 0 and h in ONES_FROM:
                    pe.wait_ge(ones_ready, i * ONES + 2 * (ONES_FROM.index(h) + 1))
                pe.wait_ge(stacked[h], i * ATT * STACK_IN + (a + 1) * STACK_IN)

            def max_pair(i, a, n):
                h, qb = divmod(n, NB)
                if qb == 0:
                    head_stacked(i, a, h)
                use = f"max{a}.{n}"
                pe.wait_ge(t_read[slot(use)], before(i, use))
                for hf in range(2):
                    last = scores_of(i, a, h, qb, hf, T[slot(use)])
                last.then_inc(t_full[slot(use)], 1)

            def max_tile(i, a, n):
                h, qb, hf = GH + n // (2 * NB), n // 2 % NB, n % 2
                if n % (2 * NB) == 0:
                    head_stacked(i, a, h)
                if a == 0 and n < 2:
                    pe.wait_ge(acc_read, i * E)
                    pe.wait_ge(stats_read, (i + 1) * 2)
                pe.wait_ge(m_read[hf], (i * ATT + a) * TILES // 2 + n // 2)
                scores_of(i, a, h, qb, hf, M).then_inc(m_full[hf], 1)

            def max_rows(i, a, g):
                use = f"rows{a}{g}"
                pe.wait_ge(t_read[slot(use)], before(i, use))
                if g == 0:
                    for n in range(GROWS - 2, GROWS):
                        pe.wait_ge(t_read[slot(f"max{a}.{n}")], filled(i, f"max{a}.{n}"))
                else:
                    pe.wait_ge(rowmax_ready, i * ATT + (a + 1))
                nc.tensor.transpose(T[slot(use)][0:GROWS, 0, 0:KB], rm[:, g * GROWS:(g + 1) * GROWS],
                                    K["ident"][0:KB, 0:KB]).then_inc(t_full[slot(use)], 1)

            def scores(i, a, g, s, pair):
                qh, kb = divmod(s, NB)
                if s == 0 and pair == 0:
                    pe.wait_ge(rowmax_in, i * ATT * NG * 48 + (a * NG + g + 1) * 48)
                use = f"s{a}{g}.{s}.{pair}"
                pe.wait_ge(t_read[slot(use)], before(i, use))
                for j in range(2):
                    h = GH * g + 2 * pair + j
                    last = mm(T[slot(use)][0:KB, j, 0:HL], stack[:, 1, h, kb * KB:(kb + 1) * KB],
                              stack[:, 0, h, qh * HL:(qh + 1) * HL])
                last.then_inc(t_full[slot(use)], 1)

            def weighted(i, a, g, s, n0=0, n1=HL):
                qh, kb = divmod(s, NB)
                if kb == 0:
                    pe.wait_ge(o_read, i * OUTS + ((a * NG + g) * 2 + qh))
                    if (a, g, qh) == (0, 0, 0):
                        pe.wait_ge(piece_read, (i + 1) * len(PIECES))
                for pair in range(2):
                    use = f"s{a}{g}.{s}.{pair}"
                    pe.wait_ge(t_read[slot(use)], filled(i, use))
                for j in range(GH):
                    last = mm(O[32 * j:32 * (j + 1), n0:n1], V[:, kb, GH * g + j, :],
                              P[pair_no(a, g, s, j // 2) % NP][:, j % 2, n0:n1], start=(kb == 0), stop=(kb == NB - 1),
                              tile_position=(0, 32 * j))
                    if j % 2 and n1 == HL:
                        last.then_inc(pv_done, 1)

            def attention(i, a, next_conv):
                fill(a, "split")
                for n in range(GROWS):
                    max_pair(i, a, n)
                    t = FILL[a]["tiles"]
                    fill(a, "tiles", (n + 1) * t // GROWS - n * t // GROWS)
                for n in range(2):
                    max_tile(i, a, n)
                max_rows(i, a, 0)
                for n in range(2, AHEAD):
                    fill(a, "rows0", 1)
                    max_tile(i, a, n)
                fill(a, "rows0", FILL[a]["rows0"] - (AHEAD - 2))
                n = AHEAD
                for s in range(STEPS):
                    for part in range(PER_STEP):
                        if part < 2:
                            scores(i, a, 0, s, part)
                        elif part == 2 and (s - 1) % NB == 0:
                            weighted(i, a, 0, s - 1)
                        elif part < 4 and s and (s - 1) % NB:
                            weighted(i, a, 0, s - 1, *((0, HL // 2), (HL // 2, HL))[part - 2])
                        if n < TILES:
                            max_tile(i, a, n)
                            n += 1
                    if s == ROWS1_STEP:
                        max_rows(i, a, 1)
                weighted(i, a, 0, STEPS - 1)
                fill(a, "rows1")
                for s in range(STEPS):
                    for pair in range(2):
                        scores(i, a, 1, s, pair)
                    if s:
                        weighted(i, a, 1, s - 1)
                weighted(i, a, 1, STEPS - 1)
                if a == 1 and next_conv:
                    first_mean(i + 1)
                use = f"out{a}"
                pe.wait_ge(t_read[slot(use)], before(i, use))
                for hf in range(2):
                    pe.wait_ge(on_ready, i * OUTS + (a + 1) * NG * 2 - (1 - hf))
                    for g in range(NG):
                        last = mm(T[slot(use)][:, hf, 0:HL], K[f"o{a}"][:, g, :], on[g][:, hf * HL:(hf + 1) * HL],
                                  start=(g == 0), stop=(g == NG - 1))
                last.then_inc(t_full[slot(use)], 1)

            def down(i, n):
                e, f = divmod(n, FB)
                if f == 0:
                    pe.wait_ge(acc_read, i * E + e)
                    if e == 0:
                        pe.wait_ge(gate_read, i + 1)
                use = f"h{e}.{f}"
                pe.wait_ge(t_read[slot(use)], filled(i, use))
                for hf in range(2):
                    last = mm(M[:, hf, 0:HL], K["w2"][:, n, :], hid[n % 3][:, hf * HL:(hf + 1) * HL],
                              start=(f == 0), stop=(f == FB - 1))
                last.then_inc(down_done, 1)

            def gate_rows(i, use, src, step):
                pe.wait_ge(t_read[slot(use)], before(i, use))
                pe.wait_ge(gate_step, i * 8 + step)
                for b in range(NB):
                    last = nc.tensor.transpose(T[slot(use)][0:E, b // 3, (b % 3) * KB:(b % 3 + 1) * KB], src[:, b, :],
                                               K["ident"][0:KB, 0:KB])
                last.then_inc(t_full[slot(use)], 1)

            def experts(i, next_conv):
                pe.wait_ge(tok_ready, i + 1)
                if next_conv:
                    pe.wait_ge(stats_read, (i + 2) * 2)
                for hf in range(2):
                    pe.wait_ge(m_read[hf], (i + 1) * ATT * TILES // 2)
                for b in range(NB):
                    last = mm(M[0:KB, 0, b * E:(b + 1) * E], tok[:, b * KB:(b + 1) * KB], K["gate_w"][:])
                last.then_inc(gate_full, 1)
                for n in range(E * FB):
                    e, f = divmod(n, FB)
                    project(i, f"h{e}.{f}", K["w1"][:, n * C:(n + 1) * C], tok)
                    if n:
                        down(i, n - 1)
                    if next_conv and n + EARLY < len(PIECES):
                        piece(i + 1, n + EARLY)
                    if n == 1:
                        gate_rows(i, "onehot", gt[:, 4], 5)
                        gate_rows(i, "weight", gt[:, 5], 8)
                    if f == 2 and e + 1 < E:
                        use = f"mask{e + 1}"
                        pe.wait_ge(t_read[slot(use)], before(i, use))
                        pe.wait_ge(t_read[slot("onehot")], filled(i, "onehot"))
                        for hf in range(2):
                            last = mm(T[slot(use)][:, hf, 0:HL], selb[:, e + 1, :], onehotT[:, hf * HL:(hf + 1) * HL])
                        last.then_inc(t_full[slot(use)], 1)
                down(i, E * FB - 1)
                pe.wait_ge(t_read[slot("weight")], filled(i, "weight"))
                project(i, "gw", K["ones8"][:], weightT)
                project(i, "b2", K["b2"][:], weightT)

            def body(i, next_conv, load_ahead):
                taps[:] = [(i + 1, half, tap) for half in range(2) for tap in range(TAPS)] if next_conv else []
                attention(i, 0, next_conv)
                pe.wait_ge(t_read[slot("out0")], filled(i, "out0"))
                layernorm(i, 1, h1)
                pe.wait_ge(n_ready, i * 2 + 1)
                for use in ("q1", "k1"):
                    project(i, use, K[use][:], nx)
                values(i)
                attention(i, 1, next_conv)
                if next_conv:
                    first_variance(i + 1)
                pe.wait_ge(t_read[slot("out1")], filled(i, "out1"))
                layernorm(i, 2, xc)
                if next_conv:
                    for n in range(EARLY):
                        piece(i + 1, n)
                experts(i, next_conv)

            pe.wait_ge(weights_split, 3)
            pe.wait_ge(consts_loaded, ALL_CONSTS)
            for half in range(2):
                for tap in range(TAPS):
                    conv_tap(0, half, tap)
            first_mean(0)
            first_variance(0)
            for n in range(len(PIECES)):
                piece(0, n)
            every_image(pe, body)

        @block.scalar
        def _(act):
            def evac_conv(m, half):
                act.wait_ge(conv_full, m * 2 + (half + 1))
                nc.scalar.activation(hc[:, half * HL:(half + 1) * HL], CV[:, 0:HL], ACT.Identity,
                                     bias=vec("conv_b")).then_inc(conv_read, 1)

            def layernorm(i, l):
                act.wait_ge(t_read[slot(f"mean{l}")], filled(i, f"mean{l}"))
                nc.scalar.activation(sq[:], xc[:], ACT.Square).then_inc(sq_ready, 1)
                use = f"var{l}"
                act.wait_ge(t_full[slot(use)], filled(i, use))
                nc.scalar.activation(halves(sq[:]), tv(use), ACT.Ln, bias=vec("eps")).then_inc(t_read[slot(use)], 1)
                act.wait_ge(t_read[slot(use)], filled(i, use))
                nc.scalar.activation(sq[:], sq[:], ACT.Exp, scale=-0.5).then_inc(rstd_ready, 1)

            def first_layernorm(m):
                act.wait_ge(stats_read, m * 2 + 1)
                nc.scalar.activation(sq0, xc0, ACT.Square).then_inc(sq0_ready, 1)
                act.wait_ge(stats_full, m * 2 + 2)
                nc.scalar.activation(halves(sq0), M[:, :, 0:HL], ACT.Ln, bias=vec("eps")).then_inc(stats_read, 1)
                act.wait_ge(stats_read, m * 2 + 2)
                nc.scalar.activation(sq0, sq0, ACT.Exp, scale=-0.5).then_inc(rstd0_ready, 1)

            def high(i, a):
                if a == 0:
                    act.wait_ge(rope_ready, i * 2 + 2)
                    act.wait_ge(piece_full, (i + 1) * len(PIECES))
                for z, name in enumerate(("q", "k")):
                    if a == 1:
                        use = f"{name}1"
                        act.wait_ge(t_full[slot(use)], filled(i, use))
                        nc.scalar.activation(halves(qk[:, z, :]), tv(use), ACT.Identity,
                                             bias=vec(use)).then_inc(t_read[slot(use)], 1)
                        act.wait_ge(t_read[slot(use)], filled(i, use))
                    nc.scalar.activation(parts[:, 3 * z, :], qk[:, z, :], ACT.Copy).then_inc(high_ready, 1)

            def middle(i, a):
                for z in range(2):
                    act.wait_ge(rest_ready, i * 2 * ATT + (2 * a + z + 1))
                    nc.scalar.activation(parts[:, 3 * z + 1, :], qk[:, z, :], ACT.Copy).then_inc(mid_ready, 1)

            def rows(i, a, g):
                use = f"rows{a}{g}"
                act.wait_ge(t_full[slot(use)], filled(i, use))
                nc.scalar.activation(rmt[:], T[slot(use)][0:GROWS, 0, 0:KB], ACT.Copy,
                                     scale=-1.0).then_inc(t_read[slot(use)], 1)

            def rows_in(i, a, g):
                act.wait_ge(ones_ready, (i + 1) * ONES)
                for part in range(3):
                    act.wait_ge(rowmax_part, i * 20 + (a * NG + g) * 5 + (2 * part + 1))
                    dst = stack[MAXROW + part:MAXROW + part + 1, 0, GH * g:GH * (g + 1), :]
                    act.dma_start(dst.rearrange("p h n -> p (h n)").rearrange("p (c q) -> p c q", q=KB),
                                  rmp[:, part, :]).then_inc(rowmax_in, 16)

            def exps(i, a, g, s):
                if g == 0 and s == 0:
                    for h in range(H):
                        act.wait_ge(stacked[h], i * ATT * STACK_IN + (a + 1) * STACK_IN)
                for pair in range(2):
                    n, use = pair_no(a, g, s, pair), f"s{a}{g}.{s}.{pair}"
                    act.wait_ge(pv_done, i * PAIRS + max(n - (NP - 1), 0))
                    act.wait_ge(t_full[slot(use)], filled(i, use))
                    nc.scalar.activation(P[n % NP][:, :, :], T[slot(use)][0:KB, :, 0:HL], ACT.Exp,
                                         scale=SCALE).then_inc(t_read[slot(use)], 1)

            def evac_out(i, k):
                act.wait_ge(pv_done, i * PAIRS + (k + 1) * 2 * NB)
                act.wait_ge(on_ready, i * OUTS + k)
                nc.scalar.activation(o_sb, O[:, 0:HL], ACT.Copy).then_inc(o_read, 1)

            def invert_sums(i, k):
                act.wait_ge(sums_ready, i * OUTS + (k + 1))
                nc.scalar.activation(sums, sums, ACT.Ln).then_inc(log_ready, 1)
                act.wait_ge(log_ready, i * OUTS + (k + 1))
                nc.scalar.activation(sums, sums, ACT.Exp, scale=-1.0).then_inc(inverse_ready, 1)

            def attention(i, a, next_conv):
                for g in range(NG):
                    k = (a * NG + g) * 2
                    if g == 0:
                        rows(i, a, 0)
                    rows_in(i, a, g)
                    for s in range(STEPS):
                        exps(i, a, g, s)
                        if s == 1 and g:
                            invert_sums(i, k - 1)
                        if s == NB:
                            evac_out(i, k)
                        if s == NB + 2:
                            invert_sums(i, k)
                        if g == 0 and s == ROWS1_STEP:
                            rows(i, a, 1)
                        if next_conv and (a, g, s) == (1, 1, 2):
                            evac_conv(i + 1, 1)
                    evac_out(i, k + 1)
                invert_sums(i, k + 1)

            def experts(i, next_conv):
                act.wait_ge(n_ready, i * 2 + 2)
                nc.scalar.activation(tok, nx[:], ACT.Identity, bias=vec("ln_b"), scale=vec("ln_g")).then_inc(tok_ready, 1)
                act.wait_ge(gate_step, i * 8 + 2)
                nc.scalar.activation(gt[:, 2], gt[:, 1], ACT.Exp).then_inc(gate_exp, 1)
                for n in range(E * FB):
                    if next_conv and n == HIGH_AT:
                        high(i + 1, 0)
                    if next_conv and n == MIDDLE_AT:
                        middle(i + 1, 0)
                    e, f = divmod(n, FB)
                    use = f"h{e}.{f}"
                    act.wait_ge(down_done, i * E * FB + max(n - 2, 0))
                    act.wait_ge(t_full[slot(use)], filled(i, use))
                    nc.scalar.activation(halves(hid[n % 3]), tv(use), ACT.Gelu_apprx_tanh,
                                         bias=K["b1"][:, n:n + 1]).then_inc(t_read[slot(use)], 1)
                    if n == 1:
                        for use, dst in (("onehot", onehotT), ("weight", weightT)):
                            act.wait_ge(t_full[slot(use)], filled(i, use))
                            nc.scalar.activation(halves(dst[:]), T[slot(use)][0:E, :, 0:HL],
                                                 ACT.Copy).then_inc(t_read[slot(use)], 1)
                    if f == 2 and e + 1 < E:
                        use = f"mask{e + 1}"
                        act.wait_ge(acc_read, i * E + e)
                        act.wait_ge(t_full[slot(use)], filled(i, use))
                        nc.scalar.activation(halves(mask[(e + 1) % 2]), tv(use), ACT.Copy).then_inc(t_read[slot(use)], 1)

            def body(i, next_conv, load_ahead):
                act.preload_act_table_set("natural_log_exp_and_others")
                attention(i, 0, next_conv)
                act.wait_ge(t_read[slot("out0")], filled(i, "out0"))
                if next_conv:
                    evac_conv(i + 1, 0)
                layernorm(i, 1)
                high(i, 1)
                middle(i, 1)
                attention(i, 1, next_conv)
                if next_conv:
                    first_layernorm(i + 1)
                layernorm(i, 2)
                experts(i, next_conv)

            act.wait_ge(consts_loaded, ALL_CONSTS)
            for half in range(2):
                evac_conv(0, half)
            first_layernorm(0)
            high(0, 0)
            middle(0, 0)
            every_image(act, body)

        @block.vector
        def _(dve):
            def split_rows(m, half):
                dve.wait_ge(conv_full, m * 2 + half)
                for c in range(CH):
                    row0, rows = CHUNKS[half][c]
                    n = CH * half + c
                    b, r = n % 2, PAD + row0 - ROW0[half]
                    dve.wait_ge(raw_in[b], m * 16 * CH + 16 * (n // 2 + 1))
                    src = raw[b][:, 0:rows, :].rearrange("p r (w s) -> p r s w", s=STRIDE)
                    hi = xh[:, r:r + rows, :, 1:1 + WI // STRIDE]
                    lo = xl[:, r:r + rows, :, 1:1 + WI // STRIDE]
                    nc.vector.tensor_copy(hi, src).then_inc(x_high, 1)
                    dve.wait_ge(x_high, m * CPI + (n + 1))
                    nc.vector.tensor_tensor(lo, src, hi.bitcast(F32), ALU.subtract).then_inc(x_split, 1)

            def centre(i, l, src):
                use = f"mean{l}"
                dve.wait_ge(t_full[slot(use)], filled(i, use))
                nc.vector.tensor_tensor(halves(xc[:]), halves(src[:]), tv(use), ALU.subtract).then_inc(t_read[slot(use)], 1)

            def normalise(i, l):
                dve.wait_ge(rstd_ready, i * 2 + l)
                nc.vector.tensor_tensor(nx[:], xc[:], sq[:], ALU.mult).then_inc(n_ready, 1)

            def first_centre(m):
                dve.wait_ge(stats_full, m * 2 + 1)
                nc.vector.tensor_tensor(halves(xc0), halves(hc[:]), M[:, :, 0:HL], ALU.subtract).then_inc(stats_read, 1)

            def first_normalise(m):
                dve.wait_ge(rstd0_ready, m + 1)
                nc.vector.tensor_tensor(nx0, xc0, sq0, ALU.mult).then_inc(n0_ready, 1)

            def piece(m, n):
                name, hf = PIECES[n]
                at = slice(hf * HL, (hf + 1) * HL)
                if n == 0:
                    dve.wait_ge(n0_ready, m + 1)
                dve.wait_ge(piece_full, m * len(PIECES) + (n + 1))
                if name == "v0":
                    add_value_bias(0, hf, O[0:KB, 0:3 * C]).then_inc(piece_read, 1)
                    return
                z = "qk".index(name[0])
                if z == 1:
                    dve.wait_ge(rope_ready, m * 2 + 1)
                table, dst = ("sin", sq0) if "p" in name else ("cos", xc0)
                nc.vector.scalar_tensor_tensor(dst[:, at], O[:, 0:HL], vec(name), K[table][:, at],
                                               ALU.add, ALU.mult).then_inc(piece_read, 1)
                if n == 4 * z + 3:
                    dve.wait_ge(piece_read, m * len(PIECES) + (n + 1))
                    nc.vector.tensor_tensor(qk[:, z, :], xc0, sq0, ALU.add).then_inc(rope_ready, 1)

            def add_value_bias(a, bank, src):
                for b in range(3):
                    last = nc.vector.tensor_tensor(
                        V[:, 3 * bank + b, :, 0:HD], src[:, b * C:(b + 1) * C].rearrange("p (h d) -> p h d", d=HD),
                        K[f"bv{a}"][:, :].rearrange("p (h d) -> p h d", d=HD), ALU.add)
                return last

            def rest(i, a, z):
                n = i * 2 * ATT + (2 * a + z + 1)
                dve.wait_ge(high_ready, n)
                nc.vector.tensor_tensor(qk[:, z, :], qk[:, z, :], parts[:, 3 * z, :], ALU.subtract).then_inc(rest_ready, 1)

            def low(i, a, z):
                n = i * 2 * ATT + (2 * a + z + 1)
                dve.wait_ge(mid_ready, n)
                nc.vector.tensor_tensor(parts[:, 3 * z + 2, :], qk[:, z, :], parts[:, 3 * z + 1, :],
                                        ALU.subtract).then_inc(low_ready, 1)

            def values(i):
                use = "v1"
                dve.wait_ge(t_full[slot(use)], filled(i, use))
                for bank in range(2):
                    last = add_value_bias(1, bank, T[slot(use)][0:KB, bank, 0:3 * C])
                last.then_inc(t_read[slot(use)], 1)

            def reduce_pair(i, a, n):
                use = f"max{a}.{n}"
                dve.wait_ge(t_full[slot(use)], filled(i, use))
                nc.vector.tensor_reduce(rm[:, n:n + 1], T[slot(use)][0:KB, :, 0:HL], AX.XY,
                                        ALU.max).then_inc(t_read[slot(use)], 1)

            def reduce_tile(i, a, n):
                hf = n % 2
                dve.wait_ge(m_full[hf], (i * ATT + a) * TILES // 2 + (n // 2 + 1))
                nc.vector.tensor_reduce(rm2[:, n // 2, hf:hf + 1], M[0:KB, hf, 0:HL], AX.X, ALU.max).then_inc(m_read[hf], 1)

            def join_halves(i, a):
                for hf in range(2):
                    dve.wait_ge(m_read[hf], (i * ATT + (a + 1)) * TILES // 2)
                nc.vector.tensor_reduce(rm[:, GROWS:2 * GROWS], rm2[:], AX.X, ALU.max).then_inc(rowmax_ready, 1)

            def row_max_parts(i, a, g):
                use = f"rows{a}{g}"
                step = i * 20 + (a * NG + g) * 5
                dve.wait_ge(t_read[slot(use)], filled(i, use))
                for part in range(3):
                    nc.vector.tensor_copy(rmp[:, part, :], rmt[:]).then_inc(rowmax_part, 1)
                    if part < 2:
                        dve.wait_ge(rowmax_part, step + (2 * part + 1))
                        nc.vector.tensor_tensor(rmt[:], rmt[:], rmp[:, part, :], ALU.subtract).then_inc(rowmax_part, 1)
                        dve.wait_ge(rowmax_part, step + (2 * part + 2))

            def spread_sums(i, k):
                dve.wait_ge(o_read, i * OUTS + (k + 1))
                hold(dve)
                nc.vector.stream_shuffle(sums, o_sb, [HD + r % HD for r in range(32)]).then_inc(sums_ready, 1)

            def scale_out(i, k):
                at = slice(k % 2 * HL, (k % 2 + 1) * HL)
                dve.wait_ge(inverse_ready, i * OUTS + (k + 1))
                nc.vector.tensor_tensor(on[1][:, at], o_sb, sums, ALU.mult).then_inc(on_ready, 1)

            def attention(i, a, next_conv):
                k = a * NG * 2
                for n in range(GROWS):
                    reduce_pair(i, a, n)
                for n in range(2):
                    reduce_tile(i, a, n)
                row_max_parts(i, a, 0)
                for n in range(2, AHEAD):
                    reduce_tile(i, a, n)
                n = AHEAD
                for s in range(STEPS):
                    for _ in range(PER_STEP):
                        if n < TILES:
                            reduce_tile(i, a, n)
                            n += 1
                            if n == TILES:
                                join_halves(i, a)
                    if s == NB + 1:
                        spread_sums(i, k)
                row_max_parts(i, a, 1)
                spread_sums(i, k + 1)
                if a == 0 and next_conv:
                    split_rows(i + 1, 1)
                for n in (k + 2, k + 3):
                    spread_sums(i, n)
                    scale_out(i, n)

            def add_out(i, a, dst, residual):
                use = f"out{a}"
                dve.wait_ge(t_full[slot(use)], filled(i, use))
                nc.vector.scalar_tensor_tensor(halves(dst[:]), tv(use), vec(f"o{a}"), halves(residual[:]),
                                               ALU.add, ALU.add).then_inc(t_read[slot(use)], 1)
                dve.wait_ge(t_read[slot(use)], filled(i, use))

            def gate(i):
                def per_token(ap):
                    return ap.unsqueeze(2).to_broadcast([KB, NB, E])

                base = i * 8
                dve.wait_ge(gate_full, i + 1)
                nc.vector.tensor_tensor(gt[:, 0], M[0:KB, 0, 0:NB * E].rearrange("p (b e) -> p b e", e=E),
                                        K["gate_b"][:], ALU.add).then_inc(gate_read, 1)
                dve.wait_ge(gate_read, i + 1)
                nc.vector.tensor_reduce(gs[:, 0], gt[:, 0], AX.X, ALU.max).then_inc(gate_step, 1)
                dve.wait_ge(gate_step, base + 1)
                nc.vector.tensor_tensor(gt[:, 1], gt[:, 0], per_token(gs[:, 0]), ALU.subtract).then_inc(gate_step, 1)
                dve.wait_ge(gate_step, base + 2)
                nc.vector.scalar_tensor_tensor(gt[:, 3], gt[:, 1], 0.0, K["key"][:], ALU.is_ge, ALU.mult).then_inc(gate_step, 1)
                dve.wait_ge(gate_step, base + 3)
                nc.vector.tensor_reduce(gs[:, 1], gt[:, 3], AX.X, ALU.max).then_inc(gate_step, 1)
                dve.wait_ge(gate_step, base + 4)
                nc.vector.tensor_tensor(gt[:, 4], gt[:, 3], per_token(gs[:, 1]), ALU.is_equal).then_inc(gate_step, 1)
                dve.wait_ge(gate_exp, i + 1)
                nc.vector.tensor_reduce(gs[:, 2], gt[:, 2], AX.X, ALU.add).then_inc(gate_step, 1)
                dve.wait_ge(gate_step, base + 6)
                nc.vector.reciprocal(gs[:, 3], gs[:, 2]).then_inc(gate_step, 1)
                dve.wait_ge(gate_step, base + 7)
                nc.vector.tensor_tensor(gt[:, 5], gt[:, 4], per_token(gs[:, 3]), ALU.mult).then_inc(gate_step, 1)

            def take_expert(i, e):
                dve.wait_ge(down_done, i * E * FB + (e + 1) * FB)
                if e == 0:
                    dve.wait_ge(stored, i * 16)
                    nc.vector.tensor_copy(halves(sel), M[:, :, 0:HL]).then_inc(acc_read, 1)
                else:
                    use = f"mask{e}"
                    dve.wait_ge(t_read[slot(use)], filled(i, use))
                    dve.wait_ge(acc_read, i * E + e)
                    hold(dve)
                    nc.vector.copy_predicated(halves(sel), halves(mask[e % 2].bitcast(U16)),
                                              M[:, :, 0:HL]).then_inc(acc_read, 1)

            def finish(i):
                dve.wait_ge(acc_read, (i + 1) * E)
                for use, op in (("gw", ALU.mult), ("b2", ALU.add)):
                    dve.wait_ge(t_full[slot(use)], filled(i, use))
                    nc.vector.tensor_tensor(halves(sel), halves(sel), tv(use), op).then_inc(t_read[slot(use)], 1)
                    dve.wait_ge(t_read[slot(use)], filled(i, use))
                nc.vector.tensor_tensor(sel, sel, h1[:], ALU.add).then_inc(y_ready, 1)

            def body(i, next_conv, load_ahead):
                attention(i, 0, next_conv)
                add_out(i, 0, h1, hc)
                centre(i, 1, h1)
                normalise(i, 1)
                rest(i, 1, 0)
                rest(i, 1, 1)
                values(i)
                low(i, 1, 0)
                low(i, 1, 1)
                attention(i, 1, next_conv)
                if next_conv:
                    first_centre(i + 1)
                add_out(i, 1, xc, nx)
                centre(i, 2, xc)
                if next_conv:
                    first_normalise(i + 1)
                    piece(i + 1, 0)
                normalise(i, 2)
                if next_conv:
                    for n in range(1, EARLY):
                        piece(i + 1, n)
                gate(i)
                for e in range(E):
                    if next_conv:
                        for n in range(EARLY + FB * e, min(EARLY + FB * (e + 1), len(PIECES))):
                            piece(i + 1, n)
                    take_expert(i, e)
                    if next_conv and e == HIGH_AT // FB:
                        for z in range(2):
                            rest(i + 1, 0, z)
                    if next_conv and e == MIDDLE_AT // FB:
                        for z in range(2):
                            low(i + 1, 0, z)
                    if load_ahead and e == MIDDLE_AT // FB + 1:
                        split_rows(i + 2, 0)
                finish(i)

            dve.wait_ge(cleared, 3)
            split_rows(0, 0)
            dve.wait_ge(conv_w_loaded, 32)
            staged = ((slice(0, BIG_TAPS), bigf[:, 0:BIG_TAPS * C]),
                      (slice(BIG_TAPS, TAPS), qk[:, :, :].rearrange("p a b -> p (a b)")[:, 0:(TAPS - BIG_TAPS) * C]))
            for n, (t, src) in enumerate(staged):
                w = src.rearrange("p (t n) -> p t n", n=C)
                nc.vector.tensor_copy(wch[:, t, :], w)
            dve.wait_ge(consts_loaded, ALL_CONSTS)
            nc.vector.tensor_copy(selb[:], parts[:, :, :].rearrange("p a b -> p (a b)").bitcast(F32)[0:E, 0:E * C].rearrange(
                "p (e n) -> p e n", n=C)).then_inc(weights_split, 1)
            dve.wait_ge(weights_split, 1)
            for n, (t, src) in enumerate(staged):
                w = src.rearrange("p (t n) -> p t n", n=C)
                nc.vector.tensor_tensor(wcl[:, t, :], w, wch[:, t, :].bitcast(F32), ALU.subtract).then_inc(weights_split, 1)
            split_rows(0, 1)
            split_rows(1, 0)
            first_centre(0)
            first_normalise(0)
            for n in range(len(PIECES)):
                piece(0, n)
            for z in range(2):
                rest(0, 0, z)
            for z in range(2):
                low(0, 0, z)
            every_image(dve, body)

        @block.gpsimd
        def _(pool):
            nc.gpsimd.memset(xh[:, :, :, :].bitcast(F32), 0.0).then_inc(cleared, 1)
            nc.gpsimd.memset(xl[:, :, :, :].bitcast(F32), 0.0).then_inc(cleared, 1)
            nc.gpsimd.memset(V[:], 1.0).then_inc(cleared, 1)

            def ones(i, step):
                heads = slice(ONES_FROM[step], (ONES_FROM + (H,))[step + 1])
                nc.gpsimd.memset(stack[SROWS:C, 0, heads, :], 0.0).then_inc(ones_ready, 1)
                nc.gpsimd.memset(stack[SROWS:C, 1, heads, :], 1.0).then_inc(ones_ready, 1)

            def body(i, next_conv, load_ahead):
                pool.wait_ge(y_ready, i)
                hold(pool)
                ones(i, 1)
                pool.wait_ge(stored, i * 16)
                hold(pool)
                ones(i, 2)
                stack_heads(pool, i, 0, range(SP_HEADS, H))
                for a in range(ATT):
                    if a:
                        stack_heads(pool, i, 1, range(SP_HEADS, H))
                    for qh in range(2):
                        k = a * NG * 2 + qh
                        pool.wait_ge(inverse_ready, i * OUTS + (k + 1))
                        nc.gpsimd.tensor_tensor(on[0][:, qh * HL:(qh + 1) * HL], o_sb, sums, ALU.mult).then_inc(on_ready, 1)
                if next_conv:
                    pool.wait_ge(tok_ready, i + 1)
                    hold(pool)
                    ones(i + 1, 0)

            pool.wait_ge(weights_split, 3)
            ones(0, 0)
            every_image(pool, body)


def layouts(p):
    n = np.arange(C)
    turned = np.where(n % 8 < 4, n + 4, n - 4)
    sign = np.where(n % 8 < 4, -1.0, 1.0).astype(np.float32)
    freq = (1.0 / np.float32(10000.0) ** (np.arange(0, HD, 2, dtype=np.float32) / np.float32(HD))).astype(np.float32)
    angle = freq[n % 8][:, None] * np.arange(L, dtype=np.float32)[None, :]

    def heads(w):
        r = np.zeros((C, NG, C), np.float32)
        for h in range(H):
            r[32 * (h % GH):32 * (h % GH) + HD, h // GH, :] = w[HD * h:HD * (h + 1), :]
        return r

    def rows(v):
        return np.broadcast_to(v, (KB, C))

    qkv, qkv_b = p["L0_attn_qkv_w"], p["L0_attn_qkv_b"]
    wq, wk, wv = (qkv[C * j:C * (j + 1)].T for j in range(3))
    bq, bk, bv = (qkv_b[C * j:C * (j + 1)] for j in range(3))
    vecs = [p["L0_tok_b"], bq, bq[turned], bk, bk[turned], p["L0_ffn_bq"], p["L0_ffn_bk"], p["L0_attn_out_b"],
            p["L0_ffn_bo"], p["L0_ffn_ln1_g"], p["L0_ffn_ln1_b"], np.full(C, EPS, np.float32)]
    consts = {
        "mean_w": np.full((C, C), 1.0 / C, np.float32), "ident": np.eye(C, dtype=np.float32),
        "cos": np.cos(angle).astype(np.float32), "sin": (np.sin(angle) * sign[:, None]).astype(np.float32),
        "key": np.broadcast_to(np.arange(E, 0, -1, dtype=np.float32), (KB, NB, E)),
        "ones8": np.ones((E, C), np.float32), "vecs": np.stack(vecs, 1),
        "b1": p["L0_ffn_b1"].reshape(E * FB, C).T,
        "q0": wq, "qp0": wq[:, turned], "k0": wk, "kp0": wk[:, turned], "v0": wv,
        "q1": p["L0_ffn_Wq"], "k1": p["L0_ffn_Wk"], "v1": p["L0_ffn_Wv"],
        "bv0": rows(bv), "bv1": rows(p["L0_ffn_bv"]),
        "o0": heads(p["L0_attn_out_w"].T), "o1": heads(p["L0_ffn_Wo"]),
        "gate_w": p["L0_ffn_gate_W"], "gate_b": np.broadcast_to(p["L0_ffn_gate_b"], (KB, NB, E)),
        "w1": p["L0_ffn_W1"].transpose(1, 0, 2).reshape(C, E * FF),
        "w2": p["L0_ffn_W2"].reshape(E * FB, C, C).transpose(1, 0, 2), "b2": p["L0_ffn_b2"],
    }
    w_conv = p["L0_tok_W"].reshape(C, C, TAPS).transpose(1, 2, 0)
    sel_rows = np.repeat(np.eye(E, dtype=np.float32), C, axis=1)
    return w_conv, sel_rows, consts


def kernel(**inputs):
    import concourse.bacc as _bacc
    from concourse.bass_utils import run_bass_kernel_spmd as _run

    p = {k: np.asarray(v) for k, v in inputs.items()}
    w_conv, sel_rows, consts = layouts(p)
    arrays = {"x": p["x"], "w_conv": w_conv, "sel_rows": sel_rows, **{f"c_{k}": v for k, v in consts.items()}}
    arrays = {k: np.ascontiguousarray(v) for k, v in arrays.items()}
    nc = _bacc.Bacc("TRN2", target_bir_lowering=False, num_devices=1)
    ap = {k: nc.dram_tensor(k, v.shape, mybir.dt.from_np(v.dtype), kind="ExternalInput").ap() for k, v in arrays.items()}
    out = nc.dram_tensor("out", (B, C, L), F32, kind="ExternalOutput").ap()
    build(nc, ap["x"], ap["w_conv"], ap["sel_rows"], {k: ap[f"c_{k}"] for k in LOADS}, out)
    r = _run(nc, [arrays], core_ids=[0])
    return np.ascontiguousarray(r.results[0]["out"].transpose(0, 2, 1))
```

```python
from contextlib import ExitStack

import numpy as np

import concourse.bass as bass
from concourse import mybir

F32 = mybir.dt.float32
F32R = mybir.dt.float32r
BF16 = mybir.dt.bfloat16
U16 = mybir.dt.uint16
ALU = mybir.AluOpType
ACT = mybir.ActivationFunctionType
AX = mybir.AxisListType

B, C, HI, WI = 16, 128, 60, 108
KH, STRIDE, PAD = 7, 3, 3
HO, WO = (HI + 2 * PAD - KH) // STRIDE + 1, (WI + 2 * PAD - KH) // STRIDE + 1
TAPS = KH * KH
L = HO * WO
HL = L // 2
H, HD = 8, C // 8
KB = 120
NB = L // KB
GH = 4
NG = H // GH
ATT = 2
STEPS = 2 * NB
GROWS = GH * NB
TILES = 2 * GROWS
SP_HEADS = 6
EARLY_HEADS = 2
ONES_FROM = (0, EARLY_HEADS, SP_HEADS)
ONES = 2 * len(ONES_FROM)
AHEAD = 8
PER_STEP = 5
ROWS1_STEP = 10
PAIRS = ATT * NG * STEPS * 2
NP = 4
OUTS = ATT * NG * 2
E, FF = 8, 4 * C
FB = FF // C
EPS = 1e-5
SCALE = 1.0 / float(HD) ** 0.5

HROWS = HO // 2
XROWS = 37
XCOLS = (WI + 2 * PAD) // STRIDE
ROW0 = (0, 27)
BASE = (0, PAD)
CHUNKS = (((0, 11), (11, 10), (21, 10)), ((27, 11), (38, 11), (49, 11)))
CH = 3
CPI = 2 * CH
RAW_ROWS = 11
BIG_TAPS = 40

TERMS = ((0, 0), (0, 1), (1, 0), (1, 1), (0, 2), (2, 0))
FIRST_LOW = 4
SROWS = HD * len(TERMS)
MAXROW = C - 3
STACK_IN = 16 * len(TERMS)


def slot_uses():
    table, used, last = {}, [0, 0, 0], 1

    def use(name, n=None):
        nonlocal last
        n = 1 - last if n is None else n
        last = last if n == 2 else n
        table[name] = (n, used[n])
        used[n] += 1

    for a in range(ATT):
        for name in ("q1", "k1", "v1") if a == 1 else ():
            use(name)
        for n in range(GROWS):
            use(f"max{a}.{n}")
        use(f"rows{a}0")
        for g in range(NG):
            for s in range(STEPS):
                for pair in range(2):
                    use(f"s{a}{g}.{s}.{pair}", (2 * s + pair) % 3 if g else None)
                if (g, s) == (0, ROWS1_STEP):
                    use(f"rows{a}1")
        for name in ("out{0}.0", "mean{1}.0", "out{0}.1", "var{1}.0", "mean{1}.1", "var{1}.1"):
            use(name.format(a, a + 1))
    for e in range(E):
        for f in range(FB):
            use(f"h{e}.{f}")
            if (e, f) == (0, 1):
                use("onehot")
                use("weight")
            if f == 2 and e + 1 < E:
                use(f"mask{e + 1}")
    use("gw")
    use("b2")
    return table, used


T_USES, T_PER = slot_uses()


def slot(use):
    return T_USES[use][0]


def filled(i, use):
    return i * T_PER[slot(use)] + (T_USES[use][1] + 1)


def before(i, use):
    return i * T_PER[slot(use)] + T_USES[use][1]


def pair_no(a, g, s, pair):
    return ((a * NG + g) * STEPS + s) * 2 + pair


LOADS = {
    "mean_w": [C, C], "ident": [C, C], "cos": [C, L], "sin": [C, L], "key": [KB, NB, E], "ones8": [E, C],
    "vecs": [C, 12], "b1": [C, E * FB], "q0": [C, C], "qp0": [C, C], "k0": [C, C], "kp0": [C, C], "v0": [C, C],
    "q1": [C, C], "k1": [C, C], "v1": [C, C], "bv0": [KB, C], "bv1": [KB, C],
    "o0": [C, NG, C], "o1": [C, NG, C], "gate_w": [C, E], "gate_b": [KB, NB, E],
    "w1": [C, E * FF], "w2": [C, E * FB, C], "b2": [E, C],
}
VEC = {n: k for k, n in enumerate(
    ["conv_b", "q0", "qp0", "k0", "kp0", "q1", "k1", "o0", "o1", "ln_g", "ln_b", "eps"])}

FILL = ({"split": 0, "tiles": 33, "rows0": 7, "rows1": TAPS},
        {"tail": 5, "mean": 2, "var": 4, "split": 20, "tiles": 4, "rows0": 7, "rows1": TAPS})

PIECES = [(name, hf) for z in "qk" for hf in range(2) for name in (f"{z}0", f"{z}p0")] + [("v0", 0), ("v0", 1)]
HIGH_AT, MIDDLE_AT = 11, 15


def build(nc, x, w_conv, sel_rows, consts, out):
    with ExitStack() as ctx:
        def sb(name, shape, dt=F32):
            return ctx.enter_context(nc.sbuf_tensor(name, shape, dt))

        def psum(name, shape):
            return ctx.enter_context(nc.psum_tensor(name, shape, F32))

        def sem(name):
            return ctx.enter_context(nc.semaphore(name))

        T = [psum(f"T{s}", [128, 2, 512]) for s in range(2)]
        T += [psum("M", [128, 2, 512])]
        M = T[2]
        O = psum("O", [128, 512])
        CV = psum("CV", [128, 512])

        def halves(ap):
            return ap.rearrange("p (a b) -> p a b", a=2)

        def cols(hf):
            return slice(hf * HL, (hf + 1) * HL)

        def th(use):
            return T[slot(use)][:, 0, 0:HL]

        def tv(use):
            return T[slot(use)][:, :, 0:HL]

        wch, wcl = sb("wch", [C, TAPS, C], F32R), sb("wcl", [C, TAPS, C], F32R)
        K = {name: sb(name, shape) for name, shape in LOADS.items()}
        selb = sb("selb", [E, E, C], BF16)

        def vec(name):
            return K["vecs"][:, VEC[name]:VEC[name] + 1]

        raw = [sb(f"raw{n}", [C, RAW_ROWS, WI]) for n in range(2)]
        xh = sb("xh", [C, XROWS, STRIDE, XCOLS], F32R)
        xl = sb("xl", [C, XROWS, STRIDE, XCOLS], F32R)
        hc, h1, nx = sb("hc", [C, L]), sb("h1", [C, L]), sb("nx", [C, L])
        xc, sq = sb("xc", [C, L]), sb("sq", [C, L])
        qk = sb("qk", [C, 2, L])
        parts = sb("parts", [C, 6, L], BF16)
        V = sb("V", [KB, NB, H, 32])
        rm2, rm = sb("rm2", [KB, GROWS, 2]), sb("rm", [KB, NG * GROWS])
        rmt, rmp = sb("rmt", [GROWS, KB]), sb("rmp", [GROWS, 3, KB], BF16)
        gt, gs = sb("gt", [KB, 6, NB, E]), sb("gs", [KB, 4, NB])
        onehotT, weightT = sb("onehotT", [E, L], BF16), sb("weightT", [E, L])
        P = [parts[:, 2 * n:2 * n + 2, :].rearrange("p a b -> p (a b)").bitcast(F32)[0:KB, :].rearrange(
            "p (j q) -> p j q", j=2) for n in range(3)] + [sq[0:KB, :].rearrange("p (j q) -> p j q", j=2)]
        xc0, sq0, nx0 = (parts[:, 2 * n:2 * n + 2, :].rearrange("p a b -> p (a b)").bitcast(F32) for n in range(3))
        big = sb("big", [128, H * 2 * L], BF16)
        stack = big[:, :].rearrange("p (s h n) -> p s h n", h=H, s=2)
        bigf = big[:, :].bitcast(F32)
        tok = bigf[:, L:2 * L]
        hid = [bigf[:, n * L:(n + 1) * L] for n in (2, 3, 5)]
        mask = [big[:, (12 + n) * L:(13 + n) * L] for n in range(2)]
        sel = bigf[:, 7 * L:8 * L]
        o_sb, sums = xc[:, 0:HL], xc[:, HL:L]
        on = [qk[:, g, :] for g in range(NG)]

        conv_w_loaded, consts_loaded = sem("conv_w_loaded"), sem("consts_loaded")
        weights_split, cleared = sem("weights_split"), sem("cleared")
        t_full, t_read = [sem(f"t_full{s}") for s in range(3)], [sem(f"t_read{s}") for s in range(3)]
        m_full, m_read = [sem(f"m_full{s}") for s in range(2)], [sem(f"m_read{s}") for s in range(2)]
        o_read = sem("o_read")
        conv_full, conv_read = sem("conv_full"), sem("conv_read")
        raw_in = [sem(f"raw_in{n}") for n in range(2)]
        x_high, x_split = sem("x_high"), sem("x_split")
        sq_ready, log_ready, rstd_ready, n_ready = sem("sq_ready"), sem("log_ready"), sem("rstd_ready"), sem("n_ready")
        stats_full, stats_read = sem("stats_full"), sem("stats_read")
        sq0_ready, rstd0_ready, n0_ready = sem("sq0_ready"), sem("rstd0_ready"), sem("n0_ready")
        piece_full, piece_read = sem("piece_full"), sem("piece_read")
        rope_ready = sem("rope_ready")
        high_ready, rest_ready, mid_ready, low_ready = (sem(f"{n}_ready") for n in ("high", "rest", "mid", "low"))
        ones_ready = sem("ones_ready")
        stacked = [sem(f"stacked{h}") for h in range(H)]
        rowmax_ready, rowmax_part, rowmax_in = sem("rowmax_ready"), sem("rowmax_part"), sem("rowmax_in")
        pv_done = sem("pv_done")
        sums_ready, inverse_ready, on_ready = sem("sums_ready"), sem("inverse_ready"), sem("on_ready")
        tok_ready = sem("tok_ready")
        gate_full, gate_read = sem("gate_full"), sem("gate_read")
        gate_step, gate_exp = sem("gate_step"), sem("gate_exp")
        down_done, acc_read = sem("down_done"), sem("acc_read")
        y_ready, stored = sem("y_ready"), sem("stored")

        held = {nc.vector.engine: sem("held_vector"), nc.gpsimd.engine: sem("held_gpsimd")}

        ALL_CONSTS = 16 * (len(LOADS) + 1)

        def hold(eng):
            eng.sem_inc(held[eng.engine], 1)

        def first(m):
            return isinstance(m, int) and m == 0

        def every_image(eng, body):
            body(0, True, True)
            with eng.Fori(1, B - 2) as i:
                body(i, True, True)
            body(B - 2, True, False)
            body(B - 1, False, False)

        def stack_heads(eng, i, a, heads):
            eng.wait_ge(mid_ready, i * 2 * ATT + (2 * a + 2))
            if eng.engine in held:
                hold(eng)
            for h in heads:
                for r, (qp, kp) in enumerate(TERMS):
                    if h == heads[0] and r == FIRST_LOW:
                        eng.wait_ge(low_ready, i * 2 * ATT + (2 * a + 2))
                        if eng.engine in held:
                            hold(eng)
                    eng.dma_start(stack[HD * r:HD * (r + 1), :, h, :],
                                  parts[HD * h:HD * (h + 1), qp:4 + kp:3 + kp - qp, :]).then_inc(stacked[h], 16)

        block = ctx.enter_context(nc.Block())

        @block.sync
        def _(sp):
            def load_rows(m, half, chunks=range(CH)):
                for c in chunks:
                    row0, rows = CHUNKS[half][c]
                    n, b = CH * half + c, (CH * half + c) % 2
                    if not (isinstance(m, int) and CPI * m + n < 2):
                        sp.wait_ge(x_split, m * CPI + (n - 1))
                    sp.dma_start(raw[b][:, 0:rows, :], x[m, :, row0:row0 + rows, :]).then_inc(raw_in[b], 16)

            load_rows(0, 0)
            sp.dma_start(bigf[:, 0:BIG_TAPS * C].rearrange("p (t n) -> p t n", n=C),
                         w_conv[:, 0:BIG_TAPS, :]).then_inc(conv_w_loaded, 16)
            sp.dma_start(qk[:, :, :].rearrange("p a b -> p (a b)")[:, 0:(TAPS - BIG_TAPS) * C].rearrange(
                "p (t n) -> p t n", n=C), w_conv[:, BIG_TAPS:TAPS, :]).then_inc(conv_w_loaded, 16)
            for name in LOADS:
                sp.dma_start(K[name][:], consts[name]).then_inc(consts_loaded, 16)
            sp.dma_start(parts[:, :, :].rearrange("p a b -> p (a b)").bitcast(F32)[0:E, 0:E * C],
                         sel_rows).then_inc(consts_loaded, 16)
            load_rows(0, 1)
            load_rows(1, 0)

            def body(i, next_conv, load_ahead):
                sp.wait_ge(y_ready, i)
                stack_heads(sp, i, 0, range(EARLY_HEADS, SP_HEADS))
                if next_conv:
                    load_rows(i + 1, 1)
                if load_ahead:
                    load_rows(i + 2, 0, range(CH - 1))
                stack_heads(sp, i, 1, range(SP_HEADS))
                if load_ahead:
                    load_rows(i + 2, 0, [CH - 1])
                if next_conv:
                    stack_heads(sp, i + 1, 0, range(EARLY_HEADS))
                sp.wait_ge(y_ready, i + 1)
                sp.dma_start(out[i], sel).then_inc(stored, 16)

            stack_heads(sp, 0, 0, range(EARLY_HEADS))
            every_image(sp, body)
            sp.wait_ge(stored, B * 16)

        @block.tensor
        def _(pe):
            def mm(out_ap, lhsT, rhs, start=True, stop=True, **kw):
                return nc.tensor.matmul(out_ap, lhsT, rhs, start=start, stop=stop, skip_group_check=True, **kw)

            def project(i, use, w, src):
                pe.wait_ge(t_read[slot(use)], before(i, use))
                for hf in range(2):
                    last = mm(T[slot(use)][0:w.shape[-1], hf, 0:HL], w, src[:, hf * HL:(hf + 1) * HL])
                last.then_inc(t_full[slot(use)], 1)

            def conv_tap(m, half, tap):
                if tap == 0:
                    pe.wait_ge(x_split, m * CPI + CH * (half + 1))
                    pe.wait_ge(conv_read, m * 2 + half)
                kh, kw = divmod(tap, KH)
                r0 = BASE[half] + kh

                def window(t):
                    return t[:, r0:r0 + STRIDE * (HROWS - 1) + 1:STRIDE, kw % STRIDE, kw // STRIDE:kw // STRIDE + WO]

                acc = CV[:, 0:HL].rearrange("p (r w) -> p r w", w=WO)
                mm(acc, wch[:, tap, :], window(xh), start=(tap == 0), stop=False)
                mm(acc, wcl[:, tap, :], window(xh), start=False, stop=False)
                last = mm(acc, wch[:, tap, :], window(xl), start=False, stop=(tap == TAPS - 1))
                if tap == TAPS - 1:
                    last.then_inc(conv_full, 1)

            taps = []

            def fill(l, place, n=None):
                floor = TAPS if l == 0 else 0
                for _ in range(max(0, min(FILL[l][place] if n is None else n, len(taps) - floor))):
                    conv_tap(*taps.pop(0))

            def mean(i, l, hf, src):
                use = f"mean{l}.{hf}"
                pe.wait_ge(t_read[slot(f"out{l - 1}.{hf}")], filled(i, f"out{l - 1}.{hf}"))
                pe.wait_ge(t_read[slot(use)], before(i, use))
                mm(th(use), K["mean_w"][:], src[:, cols(hf)]).then_inc(t_full[slot(use)], 1)

            def variance(i, l, hf):
                use = f"var{l}.{hf}"
                pe.wait_ge(sq_ready, i * 4 + (l - 1) * 2 + (hf + 1))
                pe.wait_ge(t_read[slot(use)], before(i, use))
                mm(th(use), K["mean_w"][:], sq[:, cols(hf)]).then_inc(t_full[slot(use)], 1)

            def out_half(i, a, hf):
                use = f"out{a}.{hf}"
                pe.wait_ge(on_ready, i * OUTS + (a + 1) * NG * 2 - (1 - hf))
                pe.wait_ge(t_read[slot(use)], before(i, use))
                for g in range(NG):
                    last = mm(th(use), K[f"o{a}"][:, g, :], on[g][:, cols(hf)], start=(g == 0), stop=(g == NG - 1))
                last.then_inc(t_full[slot(use)], 1)

            def values(i):
                use = "v1"
                pe.wait_ge(t_read[slot(use)], before(i, use))
                for b in range(NB):
                    last = mm(T[slot(use)][0:KB, b // 3, (b % 3) * C:(b % 3 + 1) * C],
                              nx[:, b * KB:(b + 1) * KB], K["v1"][:])
                last.then_inc(t_full[slot(use)], 1)

            def first_mean(m):
                pe.wait_ge(conv_read, m * 2 + 2)
                if not first(m):
                    pe.wait_ge(t_read[2], m * T_PER[2])
                for hf in range(2):
                    last = mm(M[:, hf, 0:HL], K["mean_w"][:], hc[:, hf * HL:(hf + 1) * HL])
                last.then_inc(stats_full, 1)

            def first_variance(m):
                pe.wait_ge(sq0_ready, m + 1)
                for hf in range(2):
                    last = mm(M[:, hf, 0:HL], K["mean_w"][:], sq0[:, hf * HL:(hf + 1) * HL])
                last.then_inc(stats_full, 1)

            def piece(m, n):
                name, hf = PIECES[n]
                if n == 0:
                    pe.wait_ge(n0_ready, m + 1)
                    if not first(m):
                        pe.wait_ge(o_read, m * OUTS)
                pe.wait_ge(piece_read, m * len(PIECES) + n)
                if name == "v0":
                    for b in range(3):
                        t = (3 * hf + b) * KB
                        last = mm(O[0:KB, b * C:(b + 1) * C], nx0[:, t:t + KB], K["v0"][:])
                else:
                    last = mm(O[:, 0:HL], K[name][:], nx0[:, hf * HL:(hf + 1) * HL])
                last.then_inc(piece_full, 1)

            def scores_of(i, a, h, qb, hf, dst):
                return mm(dst[0:KB, hf, 0:HL], stack[0:MAXROW, 0, h, qb * KB:(qb + 1) * KB],
                          stack[0:MAXROW, 1, h, hf * HL:(hf + 1) * HL])

            def head_stacked(i, a, h):
                if a == 0 and h in ONES_FROM:
                    pe.wait_ge(ones_ready, i * ONES + 2 * (ONES_FROM.index(h) + 1))
                pe.wait_ge(stacked[h], i * ATT * STACK_IN + (a + 1) * STACK_IN)

            def max_pair(i, a, n):
                h, qb = divmod(n, NB)
                if qb == 0:
                    head_stacked(i, a, h)
                use = f"max{a}.{n}"
                pe.wait_ge(t_read[slot(use)], before(i, use))
                for hf in range(2):
                    last = scores_of(i, a, h, qb, hf, T[slot(use)])
                last.then_inc(t_full[slot(use)], 1)

            def max_tile(i, a, n):
                h, qb, hf = GH + n // (2 * NB), n // 2 % NB, n % 2
                if n % (2 * NB) == 0:
                    head_stacked(i, a, h)
                if a == 0 and n < 2:
                    pe.wait_ge(acc_read, i * E)
                    pe.wait_ge(stats_read, (i + 1) * 2)
                if a == 1 and n < 2:
                    pe.wait_ge(t_read[2], i * T_PER[2] + T_PER[2] // 2)
                pe.wait_ge(m_read[hf], (i * ATT + a) * TILES // 2 + n // 2)
                scores_of(i, a, h, qb, hf, M).then_inc(m_full[hf], 1)

            def max_rows(i, a, g):
                use = f"rows{a}{g}"
                pe.wait_ge(t_read[slot(use)], before(i, use))
                if g == 0:
                    for n in range(GROWS - 2, GROWS):
                        pe.wait_ge(t_read[slot(f"max{a}.{n}")], filled(i, f"max{a}.{n}"))
                else:
                    pe.wait_ge(rowmax_ready, i * ATT + (a + 1))
                nc.tensor.transpose(T[slot(use)][0:GROWS, 0, 0:KB], rm[:, g * GROWS:(g + 1) * GROWS],
                                    K["ident"][0:KB, 0:KB]).then_inc(t_full[slot(use)], 1)

            def scores(i, a, g, s, pair):
                qh, kb = divmod(s, NB)
                if s == 0 and pair == 0:
                    pe.wait_ge(rowmax_in, i * ATT * NG * 48 + (a * NG + g + 1) * 48)
                use = f"s{a}{g}.{s}.{pair}"
                pe.wait_ge(t_read[slot(use)], before(i, use))
                if g and 2 * s + pair == 2:
                    for hf in range(2):
                        pe.wait_ge(m_read[hf], (i * ATT + (a + 1)) * TILES // 2)
                for j in range(2):
                    h = GH * g + 2 * pair + j
                    last = mm(T[slot(use)][0:KB, j, 0:HL], stack[:, 1, h, kb * KB:(kb + 1) * KB],
                              stack[:, 0, h, qh * HL:(qh + 1) * HL])
                last.then_inc(t_full[slot(use)], 1)

            def weighted(i, a, g, s, n0=0, n1=HL):
                qh, kb = divmod(s, NB)
                if kb == 0:
                    pe.wait_ge(o_read, i * OUTS + ((a * NG + g) * 2 + qh))
                    if (a, g, qh) == (0, 0, 0):
                        pe.wait_ge(piece_read, (i + 1) * len(PIECES))
                for pair in range(2):
                    use = f"s{a}{g}.{s}.{pair}"
                    pe.wait_ge(t_read[slot(use)], filled(i, use))
                for j in range(GH):
                    last = mm(O[32 * j:32 * (j + 1), n0:n1], V[:, kb, GH * g + j, :],
                              P[pair_no(a, g, s, j // 2) % NP][:, j % 2, n0:n1], start=(kb == 0), stop=(kb == NB - 1),
                              tile_position=(0, 32 * j))
                    if j % 2 and n1 == HL:
                        last.then_inc(pv_done, 1)

            def attention(i, a, next_conv):
                fill(a, "split")
                for n in range(GROWS):
                    max_pair(i, a, n)
                    t = FILL[a]["tiles"]
                    fill(a, "tiles", (n + 1) * t // GROWS - n * t // GROWS)
                for n in range(2):
                    max_tile(i, a, n)
                max_rows(i, a, 0)
                for n in range(2, AHEAD):
                    fill(a, "rows0", 1)
                    max_tile(i, a, n)
                fill(a, "rows0", FILL[a]["rows0"] - (AHEAD - 2))
                n = AHEAD
                for s in range(STEPS):
                    for part in range(PER_STEP):
                        if part < 2:
                            scores(i, a, 0, s, part)
                        elif part == 2 and (s - 1) % NB == 0:
                            weighted(i, a, 0, s - 1)
                        elif part < 4 and s and (s - 1) % NB:
                            weighted(i, a, 0, s - 1, *((0, HL // 2), (HL // 2, HL))[part - 2])
                        if n < TILES:
                            max_tile(i, a, n)
                            n += 1
                    if s == ROWS1_STEP:
                        max_rows(i, a, 1)
                weighted(i, a, 0, STEPS - 1)
                fill(a, "rows1")
                for s in range(STEPS):
                    for pair in range(2):
                        scores(i, a, 1, s, pair)
                    if s:
                        weighted(i, a, 1, s - 1)
                weighted(i, a, 1, STEPS - 1)
                out_half(i, a, 0)
                l, src = a + 1, (h1, nx)[a]
                mean(i, l, 0, src)
                if next_conv and a == 1:
                    first_mean(i + 1)
                if a == 0:
                    fill(1, "tail")
                out_half(i, a, 1)
                variance(i, l, 0)
                if a == 0:
                    fill(1, "mean")
                mean(i, l, 1, src)
                if a == 0:
                    fill(1, "var")
                elif next_conv:
                    first_variance(i + 1)
                variance(i, l, 1)

            def down(i, n):
                e, f = divmod(n, FB)
                if f == 0:
                    pe.wait_ge(acc_read, i * E + e)
                    if e == 0:
                        pe.wait_ge(gate_read, i + 1)
                use = f"h{e}.{f}"
                pe.wait_ge(t_read[slot(use)], filled(i, use))
                for hf in range(2):
                    last = mm(M[:, hf, 0:HL], K["w2"][:, n, :], hid[n % 3][:, hf * HL:(hf + 1) * HL],
                              start=(f == 0), stop=(f == FB - 1))
                last.then_inc(down_done, 1)

            def gate_rows(i, use, src, step):
                pe.wait_ge(t_read[slot(use)], before(i, use))
                pe.wait_ge(gate_step, i * 8 + step)
                for b in range(NB):
                    last = nc.tensor.transpose(T[slot(use)][0:E, b // 3, (b % 3) * KB:(b % 3 + 1) * KB], src[:, b, :],
                                               K["ident"][0:KB, 0:KB])
                last.then_inc(t_full[slot(use)], 1)

            def experts(i, next_conv):
                if next_conv:
                    pe.wait_ge(stats_read, (i + 2) * 2)
                pe.wait_ge(t_read[2], (i + 1) * T_PER[2])
                for b in range(NB):
                    if b % 3 == 0:
                        pe.wait_ge(tok_ready, i * 2 + (b // 3 + 1))
                    last = mm(M[0:KB, 0, b * E:(b + 1) * E], tok[:, b * KB:(b + 1) * KB], K["gate_w"][:])
                last.then_inc(gate_full, 1)
                for n in range(E * FB):
                    e, f = divmod(n, FB)
                    project(i, f"h{e}.{f}", K["w1"][:, n * C:(n + 1) * C], tok)
                    if n:
                        down(i, n - 1)
                    if next_conv and n < len(PIECES):
                        piece(i + 1, n)
                    if n == 1:
                        gate_rows(i, "onehot", gt[:, 4], 5)
                        gate_rows(i, "weight", gt[:, 5], 8)
                    if f == 2 and e + 1 < E:
                        use = f"mask{e + 1}"
                        pe.wait_ge(t_read[slot(use)], before(i, use))
                        pe.wait_ge(t_read[slot("onehot")], filled(i, "onehot"))
                        for hf in range(2):
                            last = mm(T[slot(use)][:, hf, 0:HL], selb[:, e + 1, :], onehotT[:, hf * HL:(hf + 1) * HL])
                        last.then_inc(t_full[slot(use)], 1)
                down(i, E * FB - 1)
                pe.wait_ge(t_read[slot("weight")], filled(i, "weight"))
                project(i, "gw", K["ones8"][:], weightT)
                project(i, "b2", K["b2"][:], weightT)

            def body(i, next_conv, load_ahead):
                taps[:] = [(i + 1, half, tap) for half in range(2) for tap in range(TAPS)] if next_conv else []
                attention(i, 0, next_conv)
                for use in ("q1", "k1"):
                    pe.wait_ge(t_read[slot(use)], before(i, use))
                    for hf in range(2):
                        pe.wait_ge(n_ready, i * 4 + (hf + 1))
                        last = mm(T[slot(use)][:, hf, 0:HL], K[use][:], nx[:, cols(hf)])
                    last.then_inc(t_full[slot(use)], 1)
                values(i)
                attention(i, 1, next_conv)
                experts(i, next_conv)

            pe.wait_ge(weights_split, 3)
            pe.wait_ge(consts_loaded, ALL_CONSTS)
            for half in range(2):
                for tap in range(TAPS):
                    conv_tap(0, half, tap)
            first_mean(0)
            first_variance(0)
            for n in range(len(PIECES)):
                piece(0, n)
            every_image(pe, body)

        @block.scalar
        def _(act):
            def evac_conv(m, half):
                act.wait_ge(conv_full, m * 2 + (half + 1))
                nc.scalar.activation(hc[:, half * HL:(half + 1) * HL], CV[:, 0:HL], ACT.Identity,
                                     bias=vec("conv_b")).then_inc(conv_read, 1)

            def square(i, l, hf):
                use = f"mean{l}.{hf}"
                act.wait_ge(t_read[slot(use)], filled(i, use))
                nc.scalar.activation(sq[:, cols(hf)], xc[:, cols(hf)], ACT.Square).then_inc(sq_ready, 1)

            def inverse_deviation(i, l, hf):
                use, at = f"var{l}.{hf}", cols(hf)
                act.wait_ge(t_full[slot(use)], filled(i, use))
                nc.scalar.activation(sq[:, at], th(use), ACT.Ln, bias=vec("eps")).then_inc(t_read[slot(use)], 1)
                act.wait_ge(t_read[slot(use)], filled(i, use))
                nc.scalar.activation(sq[:, at], sq[:, at], ACT.Exp, scale=-0.5).then_inc(rstd_ready, 1)

            def tokens(i, hf):
                act.wait_ge(n_ready, i * 4 + 2 + (hf + 1))
                nc.scalar.activation(tok[:, cols(hf)], nx[:, cols(hf)], ACT.Identity, bias=vec("ln_b"),
                                     scale=vec("ln_g")).then_inc(tok_ready, 1)

            def first_square(m):
                act.wait_ge(stats_read, m * 2 + 1)
                nc.scalar.activation(sq0, xc0, ACT.Square).then_inc(sq0_ready, 1)

            def first_log(m):
                act.wait_ge(stats_full, m * 2 + 2)
                nc.scalar.activation(halves(sq0), M[:, :, 0:HL], ACT.Ln, bias=vec("eps")).then_inc(stats_read, 1)

            def first_inverse_deviation(m):
                act.wait_ge(stats_read, m * 2 + 2)
                nc.scalar.activation(sq0, sq0, ACT.Exp, scale=-0.5).then_inc(rstd0_ready, 1)

            def high(i, a):
                if a == 0:
                    act.wait_ge(rope_ready, i * 2 + 2)
                    act.wait_ge(piece_full, (i + 1) * len(PIECES))
                for z, name in enumerate(("q", "k")):
                    if a == 1:
                        use = f"{name}1"
                        act.wait_ge(t_full[slot(use)], filled(i, use))
                        nc.scalar.activation(halves(qk[:, z, :]), tv(use), ACT.Identity,
                                             bias=vec(use)).then_inc(t_read[slot(use)], 1)
                        act.wait_ge(t_read[slot(use)], filled(i, use))
                    nc.scalar.activation(parts[:, 3 * z, :], qk[:, z, :], ACT.Copy).then_inc(high_ready, 1)

            def middle(i, a):
                for z in range(2):
                    act.wait_ge(rest_ready, i * 2 * ATT + (2 * a + z + 1))
                    nc.scalar.activation(parts[:, 3 * z + 1, :], qk[:, z, :], ACT.Copy).then_inc(mid_ready, 1)

            def rows(i, a, g):
                use = f"rows{a}{g}"
                act.wait_ge(t_full[slot(use)], filled(i, use))
                nc.scalar.activation(rmt[:], T[slot(use)][0:GROWS, 0, 0:KB], ACT.Copy,
                                     scale=-1.0).then_inc(t_read[slot(use)], 1)

            def rows_in(i, a, g):
                act.wait_ge(ones_ready, (i + 1) * ONES)
                for part in range(3):
                    act.wait_ge(rowmax_part, i * 20 + (a * NG + g) * 5 + (2 * part + 1))
                    dst = stack[MAXROW + part:MAXROW + part + 1, 0, GH * g:GH * (g + 1), :]
                    act.dma_start(dst.rearrange("p h n -> p (h n)").rearrange("p (c q) -> p c q", q=KB),
                                  rmp[:, part, :]).then_inc(rowmax_in, 16)

            def exps(i, a, g, s):
                if g == 0 and s == 0:
                    for h in range(H):
                        act.wait_ge(stacked[h], i * ATT * STACK_IN + (a + 1) * STACK_IN)
                for pair in range(2):
                    n, use = pair_no(a, g, s, pair), f"s{a}{g}.{s}.{pair}"
                    act.wait_ge(pv_done, i * PAIRS + max(n - (NP - 1), 0))
                    act.wait_ge(t_full[slot(use)], filled(i, use))
                    nc.scalar.activation(P[n % NP][:, :, :], T[slot(use)][0:KB, :, 0:HL], ACT.Exp,
                                         scale=SCALE).then_inc(t_read[slot(use)], 1)

            def evac_out(i, k):
                act.wait_ge(pv_done, i * PAIRS + (k + 1) * 2 * NB)
                act.wait_ge(on_ready, i * OUTS + k)
                nc.scalar.activation(o_sb, O[:, 0:HL], ACT.Copy).then_inc(o_read, 1)

            def invert_sums(i, k):
                act.wait_ge(sums_ready, i * OUTS + (k + 1))
                nc.scalar.activation(sums, sums, ACT.Ln).then_inc(log_ready, 1)
                act.wait_ge(log_ready, i * OUTS + (k + 1))
                nc.scalar.activation(sums, sums, ACT.Exp, scale=-1.0).then_inc(inverse_ready, 1)

            def attention(i, a, next_conv):
                for g in range(NG):
                    k = (a * NG + g) * 2
                    if g == 0:
                        rows(i, a, 0)
                    rows_in(i, a, g)
                    for s in range(STEPS):
                        exps(i, a, g, s)
                        if s == 1 and g:
                            invert_sums(i, k - 1)
                        if s == NB:
                            evac_out(i, k)
                        if s == NB + 2:
                            invert_sums(i, k)
                        if g == 0 and s == ROWS1_STEP:
                            rows(i, a, 1)
                        if next_conv and (a, g, s) == (1, 1, 2):
                            evac_conv(i + 1, 1)
                    evac_out(i, k + 1)
                invert_sums(i, k + 1)
                if next_conv and a == 0:
                    act.wait_ge(t_read[slot("out0.0")], filled(i, "out0.0"))
                    evac_conv(i + 1, 0)

            def experts(i, next_conv):
                act.wait_ge(gate_step, i * 8 + 2)
                nc.scalar.activation(gt[:, 2], gt[:, 1], ACT.Exp).then_inc(gate_exp, 1)
                for n in range(E * FB):
                    if next_conv and n == HIGH_AT:
                        high(i + 1, 0)
                    if next_conv and n == MIDDLE_AT:
                        middle(i + 1, 0)
                    e, f = divmod(n, FB)
                    use = f"h{e}.{f}"
                    act.wait_ge(down_done, i * E * FB + max(n - 2, 0))
                    act.wait_ge(t_full[slot(use)], filled(i, use))
                    nc.scalar.activation(halves(hid[n % 3]), tv(use), ACT.Gelu_apprx_tanh,
                                         bias=K["b1"][:, n:n + 1]).then_inc(t_read[slot(use)], 1)
                    if n == 1:
                        for use, dst in (("onehot", onehotT), ("weight", weightT)):
                            act.wait_ge(t_full[slot(use)], filled(i, use))
                            nc.scalar.activation(halves(dst[:]), T[slot(use)][0:E, :, 0:HL],
                                                 ACT.Copy).then_inc(t_read[slot(use)], 1)
                    if f == 2 and e + 1 < E:
                        use = f"mask{e + 1}"
                        act.wait_ge(acc_read, i * E + e)
                        act.wait_ge(t_full[slot(use)], filled(i, use))
                        nc.scalar.activation(halves(mask[(e + 1) % 2]), tv(use), ACT.Copy).then_inc(t_read[slot(use)], 1)

            def body(i, next_conv, load_ahead):
                act.preload_act_table_set("natural_log_exp_and_others")
                attention(i, 0, next_conv)
                square(i, 1, 0)
                inverse_deviation(i, 1, 0)
                square(i, 1, 1)
                inverse_deviation(i, 1, 1)
                high(i, 1)
                middle(i, 1)
                attention(i, 1, next_conv)
                square(i, 2, 0)
                if next_conv:
                    first_square(i + 1)
                inverse_deviation(i, 2, 0)
                square(i, 2, 1)
                tokens(i, 0)
                if next_conv:
                    first_log(i + 1)
                inverse_deviation(i, 2, 1)
                tokens(i, 1)
                if next_conv:
                    first_inverse_deviation(i + 1)
                experts(i, next_conv)

            act.wait_ge(consts_loaded, ALL_CONSTS)
            for half in range(2):
                evac_conv(0, half)
            first_square(0)
            first_log(0)
            first_inverse_deviation(0)
            high(0, 0)
            middle(0, 0)
            every_image(act, body)

        @block.vector
        def _(dve):
            def split_rows(m, half):
                dve.wait_ge(conv_full, m * 2 + half)
                for c in range(CH):
                    row0, rows = CHUNKS[half][c]
                    n = CH * half + c
                    b, r = n % 2, PAD + row0 - ROW0[half]
                    dve.wait_ge(raw_in[b], m * 16 * CH + 16 * (n // 2 + 1))
                    src = raw[b][:, 0:rows, :].rearrange("p r (w s) -> p r s w", s=STRIDE)
                    hi = xh[:, r:r + rows, :, 1:1 + WI // STRIDE]
                    lo = xl[:, r:r + rows, :, 1:1 + WI // STRIDE]
                    nc.vector.tensor_copy(hi, src).then_inc(x_high, 1)
                    dve.wait_ge(x_high, m * CPI + (n + 1))
                    nc.vector.tensor_tensor(lo, src, hi.bitcast(F32), ALU.subtract).then_inc(x_split, 1)

            def centre(i, l, hf, src):
                use = f"mean{l}.{hf}"
                dve.wait_ge(on_ready, i * OUTS + l * NG * 2)
                dve.wait_ge(t_full[slot(use)], filled(i, use))
                nc.vector.tensor_tensor(xc[:, cols(hf)], src[:, cols(hf)], th(use), ALU.subtract).then_inc(t_read[slot(use)], 1)

            def normalise(i, l, hf):
                dve.wait_ge(rstd_ready, i * 4 + (l - 1) * 2 + (hf + 1))
                nc.vector.tensor_tensor(nx[:, cols(hf)], xc[:, cols(hf)], sq[:, cols(hf)], ALU.mult).then_inc(n_ready, 1)

            def first_centre(m):
                dve.wait_ge(stats_full, m * 2 + 1)
                nc.vector.tensor_tensor(halves(xc0), halves(hc[:]), M[:, :, 0:HL], ALU.subtract).then_inc(stats_read, 1)

            def first_normalise(m):
                dve.wait_ge(rstd0_ready, m + 1)
                nc.vector.tensor_tensor(nx0, xc0, sq0, ALU.mult).then_inc(n0_ready, 1)

            def piece(m, n):
                name, hf = PIECES[n]
                at = slice(hf * HL, (hf + 1) * HL)
                if n == 0:
                    dve.wait_ge(n0_ready, m + 1)
                dve.wait_ge(piece_full, m * len(PIECES) + (n + 1))
                if name == "v0":
                    add_value_bias(0, hf, O[0:KB, 0:3 * C]).then_inc(piece_read, 1)
                    return
                z = "qk".index(name[0])
                if z == 1:
                    dve.wait_ge(rope_ready, m * 2 + 1)
                table, dst = ("sin", sq0) if "p" in name else ("cos", xc0)
                nc.vector.scalar_tensor_tensor(dst[:, at], O[:, 0:HL], vec(name), K[table][:, at],
                                               ALU.add, ALU.mult).then_inc(piece_read, 1)
                if n == 4 * z + 3:
                    dve.wait_ge(piece_read, m * len(PIECES) + (n + 1))
                    nc.vector.tensor_tensor(qk[:, z, :], xc0, sq0, ALU.add).then_inc(rope_ready, 1)

            def add_value_bias(a, bank, src):
                for b in range(3):
                    last = nc.vector.tensor_tensor(
                        V[:, 3 * bank + b, :, 0:HD], src[:, b * C:(b + 1) * C].rearrange("p (h d) -> p h d", d=HD),
                        K[f"bv{a}"][:, :].rearrange("p (h d) -> p h d", d=HD), ALU.add)
                return last

            def rest(i, a, z):
                n = i * 2 * ATT + (2 * a + z + 1)
                dve.wait_ge(high_ready, n)
                nc.vector.tensor_tensor(qk[:, z, :], qk[:, z, :], parts[:, 3 * z, :], ALU.subtract).then_inc(rest_ready, 1)

            def low(i, a, z):
                n = i * 2 * ATT + (2 * a + z + 1)
                dve.wait_ge(mid_ready, n)
                nc.vector.tensor_tensor(parts[:, 3 * z + 2, :], qk[:, z, :], parts[:, 3 * z + 1, :],
                                        ALU.subtract).then_inc(low_ready, 1)

            def values(i):
                use = "v1"
                dve.wait_ge(t_full[slot(use)], filled(i, use))
                for bank in range(2):
                    last = add_value_bias(1, bank, T[slot(use)][0:KB, bank, 0:3 * C])
                last.then_inc(t_read[slot(use)], 1)

            def reduce_pair(i, a, n):
                use = f"max{a}.{n}"
                dve.wait_ge(t_full[slot(use)], filled(i, use))
                nc.vector.tensor_reduce(rm[:, n:n + 1], T[slot(use)][0:KB, :, 0:HL], AX.XY,
                                        ALU.max).then_inc(t_read[slot(use)], 1)

            def reduce_tile(i, a, n):
                hf = n % 2
                dve.wait_ge(m_full[hf], (i * ATT + a) * TILES // 2 + (n // 2 + 1))
                nc.vector.tensor_reduce(rm2[:, n // 2, hf:hf + 1], M[0:KB, hf, 0:HL], AX.X, ALU.max).then_inc(m_read[hf], 1)

            def join_halves(i, a):
                for hf in range(2):
                    dve.wait_ge(m_read[hf], (i * ATT + (a + 1)) * TILES // 2)
                nc.vector.tensor_reduce(rm[:, GROWS:2 * GROWS], rm2[:], AX.X, ALU.max).then_inc(rowmax_ready, 1)

            def row_max_parts(i, a, g):
                use = f"rows{a}{g}"
                step = i * 20 + (a * NG + g) * 5
                dve.wait_ge(t_read[slot(use)], filled(i, use))
                for part in range(3):
                    nc.vector.tensor_copy(rmp[:, part, :], rmt[:]).then_inc(rowmax_part, 1)
                    if part < 2:
                        dve.wait_ge(rowmax_part, step + (2 * part + 1))
                        nc.vector.tensor_tensor(rmt[:], rmt[:], rmp[:, part, :], ALU.subtract).then_inc(rowmax_part, 1)
                        dve.wait_ge(rowmax_part, step + (2 * part + 2))

            def spread_sums(i, k):
                dve.wait_ge(o_read, i * OUTS + (k + 1))
                hold(dve)
                nc.vector.stream_shuffle(sums, o_sb, [HD + r % HD for r in range(32)]).then_inc(sums_ready, 1)

            def scale_out(i, k):
                at = slice(k % 2 * HL, (k % 2 + 1) * HL)
                dve.wait_ge(inverse_ready, i * OUTS + (k + 1))
                nc.vector.tensor_tensor(on[1][:, at], o_sb, sums, ALU.mult).then_inc(on_ready, 1)

            def attention(i, a, next_conv):
                k = a * NG * 2
                for n in range(GROWS):
                    reduce_pair(i, a, n)
                for n in range(2):
                    reduce_tile(i, a, n)
                row_max_parts(i, a, 0)
                for n in range(2, AHEAD):
                    reduce_tile(i, a, n)
                n = AHEAD
                for s in range(STEPS):
                    for _ in range(PER_STEP):
                        if n < TILES:
                            reduce_tile(i, a, n)
                            n += 1
                            if n == TILES:
                                join_halves(i, a)
                    if s == NB + 1:
                        spread_sums(i, k)
                row_max_parts(i, a, 1)
                spread_sums(i, k + 1)
                if a == 0 and next_conv:
                    split_rows(i + 1, 1)
                l, dst, residual = a + 1, (h1, nx)[a], (hc, nx)[a]
                spread_sums(i, k + 2)
                scale_out(i, k + 2)
                spread_sums(i, k + 3)
                add_out(i, a, 0, dst, residual)
                scale_out(i, k + 3)
                centre(i, l, 0, dst)
                if next_conv and a == 1:
                    first_centre(i + 1)
                add_out(i, a, 1, dst, residual)
                centre(i, l, 1, dst)
                normalise(i, l, 0)
                normalise(i, l, 1)

            def add_out(i, a, hf, dst, residual):
                use = f"out{a}.{hf}"
                dve.wait_ge(t_full[slot(use)], filled(i, use))
                nc.vector.scalar_tensor_tensor(dst[:, cols(hf)], th(use), vec(f"o{a}"), residual[:, cols(hf)],
                                               ALU.add, ALU.add).then_inc(t_read[slot(use)], 1)
                dve.wait_ge(t_read[slot(use)], filled(i, use))

            def gate(i):
                def per_token(ap):
                    return ap.unsqueeze(2).to_broadcast([KB, NB, E])

                base = i * 8
                dve.wait_ge(gate_full, i + 1)
                nc.vector.tensor_tensor(gt[:, 0], M[0:KB, 0, 0:NB * E].rearrange("p (b e) -> p b e", e=E),
                                        K["gate_b"][:], ALU.add).then_inc(gate_read, 1)
                dve.wait_ge(gate_read, i + 1)
                nc.vector.tensor_reduce(gs[:, 0], gt[:, 0], AX.X, ALU.max).then_inc(gate_step, 1)
                dve.wait_ge(gate_step, base + 1)
                nc.vector.tensor_tensor(gt[:, 1], gt[:, 0], per_token(gs[:, 0]), ALU.subtract).then_inc(gate_step, 1)
                dve.wait_ge(gate_step, base + 2)
                nc.vector.scalar_tensor_tensor(gt[:, 3], gt[:, 1], 0.0, K["key"][:], ALU.is_ge, ALU.mult).then_inc(gate_step, 1)
                dve.wait_ge(gate_step, base + 3)
                nc.vector.tensor_reduce(gs[:, 1], gt[:, 3], AX.X, ALU.max).then_inc(gate_step, 1)
                dve.wait_ge(gate_step, base + 4)
                nc.vector.tensor_tensor(gt[:, 4], gt[:, 3], per_token(gs[:, 1]), ALU.is_equal).then_inc(gate_step, 1)
                dve.wait_ge(gate_exp, i + 1)
                nc.vector.tensor_reduce(gs[:, 2], gt[:, 2], AX.X, ALU.add).then_inc(gate_step, 1)
                dve.wait_ge(gate_step, base + 6)
                nc.vector.reciprocal(gs[:, 3], gs[:, 2]).then_inc(gate_step, 1)
                dve.wait_ge(gate_step, base + 7)
                nc.vector.tensor_tensor(gt[:, 5], gt[:, 4], per_token(gs[:, 3]), ALU.mult).then_inc(gate_step, 1)

            def take_expert(i, e):
                dve.wait_ge(down_done, i * E * FB + (e + 1) * FB)
                if e == 0:
                    dve.wait_ge(stored, i * 16)
                    nc.vector.tensor_copy(halves(sel), M[:, :, 0:HL]).then_inc(acc_read, 1)
                else:
                    use = f"mask{e}"
                    dve.wait_ge(t_read[slot(use)], filled(i, use))
                    dve.wait_ge(acc_read, i * E + e)
                    hold(dve)
                    nc.vector.copy_predicated(halves(sel), halves(mask[e % 2].bitcast(U16)),
                                              M[:, :, 0:HL]).then_inc(acc_read, 1)

            def finish(i):
                dve.wait_ge(acc_read, (i + 1) * E)
                for use, op in (("gw", ALU.mult), ("b2", ALU.add)):
                    dve.wait_ge(t_full[slot(use)], filled(i, use))
                    nc.vector.tensor_tensor(halves(sel), halves(sel), tv(use), op).then_inc(t_read[slot(use)], 1)
                    dve.wait_ge(t_read[slot(use)], filled(i, use))
                nc.vector.tensor_tensor(sel, sel, h1[:], ALU.add).then_inc(y_ready, 1)

            def body(i, next_conv, load_ahead):
                attention(i, 0, next_conv)
                rest(i, 1, 0)
                rest(i, 1, 1)
                values(i)
                low(i, 1, 0)
                low(i, 1, 1)
                attention(i, 1, next_conv)
                gate(i)
                if next_conv:
                    first_normalise(i + 1)
                for e in range(E):
                    if next_conv:
                        for n in range(FB * e, min(FB * (e + 1), len(PIECES))):
                            piece(i + 1, n)
                    take_expert(i, e)
                    if next_conv and e == HIGH_AT // FB:
                        for z in range(2):
                            rest(i + 1, 0, z)
                    if next_conv and e == MIDDLE_AT // FB:
                        for z in range(2):
                            low(i + 1, 0, z)
                    if load_ahead and e == MIDDLE_AT // FB + 1:
                        split_rows(i + 2, 0)
                finish(i)

            dve.wait_ge(cleared, 3)
            split_rows(0, 0)
            dve.wait_ge(conv_w_loaded, 32)
            staged = ((slice(0, BIG_TAPS), bigf[:, 0:BIG_TAPS * C]),
                      (slice(BIG_TAPS, TAPS), qk[:, :, :].rearrange("p a b -> p (a b)")[:, 0:(TAPS - BIG_TAPS) * C]))
            for n, (t, src) in enumerate(staged):
                w = src.rearrange("p (t n) -> p t n", n=C)
                nc.vector.tensor_copy(wch[:, t, :], w)
            dve.wait_ge(consts_loaded, ALL_CONSTS)
            nc.vector.tensor_copy(selb[:], parts[:, :, :].rearrange("p a b -> p (a b)").bitcast(F32)[0:E, 0:E * C].rearrange(
                "p (e n) -> p e n", n=C)).then_inc(weights_split, 1)
            dve.wait_ge(weights_split, 1)
            for n, (t, src) in enumerate(staged):
                w = src.rearrange("p (t n) -> p t n", n=C)
                nc.vector.tensor_tensor(wcl[:, t, :], w, wch[:, t, :].bitcast(F32), ALU.subtract).then_inc(weights_split, 1)
            split_rows(0, 1)
            split_rows(1, 0)
            first_centre(0)
            first_normalise(0)
            for n in range(len(PIECES)):
                piece(0, n)
            for z in range(2):
                rest(0, 0, z)
            for z in range(2):
                low(0, 0, z)
            every_image(dve, body)

        @block.gpsimd
        def _(pool):
            nc.gpsimd.memset(xh[:, :, :, :].bitcast(F32), 0.0).then_inc(cleared, 1)
            nc.gpsimd.memset(xl[:, :, :, :].bitcast(F32), 0.0).then_inc(cleared, 1)
            nc.gpsimd.memset(V[:], 1.0).then_inc(cleared, 1)

            def ones(i, step):
                heads = slice(ONES_FROM[step], (ONES_FROM + (H,))[step + 1])
                nc.gpsimd.memset(stack[SROWS:C, 0, heads, :], 0.0).then_inc(ones_ready, 1)
                nc.gpsimd.memset(stack[SROWS:C, 1, heads, :], 1.0).then_inc(ones_ready, 1)

            def body(i, next_conv, load_ahead):
                pool.wait_ge(y_ready, i)
                hold(pool)
                ones(i, 1)
                pool.wait_ge(stored, i * 16)
                hold(pool)
                ones(i, 2)
                stack_heads(pool, i, 0, range(SP_HEADS, H))
                for a in range(ATT):
                    if a:
                        stack_heads(pool, i, 1, range(SP_HEADS, H))
                    for qh in range(2):
                        k = a * NG * 2 + qh
                        pool.wait_ge(inverse_ready, i * OUTS + (k + 1))
                        nc.gpsimd.tensor_tensor(on[0][:, qh * HL:(qh + 1) * HL], o_sb, sums, ALU.mult).then_inc(on_ready, 1)
                if next_conv:
                    pool.wait_ge(tok_ready, i * 2 + 2)
                    hold(pool)
                    ones(i + 1, 0)

            pool.wait_ge(weights_split, 3)
            ones(0, 0)
            every_image(pool, body)


def layouts(p):
    n = np.arange(C)
    turned = np.where(n % 8 < 4, n + 4, n - 4)
    sign = np.where(n % 8 < 4, -1.0, 1.0).astype(np.float32)
    freq = (1.0 / np.float32(10000.0) ** (np.arange(0, HD, 2, dtype=np.float32) / np.float32(HD))).astype(np.float32)
    angle = freq[n % 8][:, None] * np.arange(L, dtype=np.float32)[None, :]

    def heads(w):
        r = np.zeros((C, NG, C), np.float32)
        for h in range(H):
            r[32 * (h % GH):32 * (h % GH) + HD, h // GH, :] = w[HD * h:HD * (h + 1), :]
        return r

    def rows(v):
        return np.broadcast_to(v, (KB, C))

    qkv, qkv_b = p["L0_attn_qkv_w"], p["L0_attn_qkv_b"]
    wq, wk, wv = (qkv[C * j:C * (j + 1)].T for j in range(3))
    bq, bk, bv = (qkv_b[C * j:C * (j + 1)] for j in range(3))
    vecs = [p["L0_tok_b"], bq, bq[turned], bk, bk[turned], p["L0_ffn_bq"], p["L0_ffn_bk"], p["L0_attn_out_b"],
            p["L0_ffn_bo"], p["L0_ffn_ln1_g"], p["L0_ffn_ln1_b"], np.full(C, EPS, np.float32)]
    consts = {
        "mean_w": np.full((C, C), 1.0 / C, np.float32), "ident": np.eye(C, dtype=np.float32),
        "cos": np.cos(angle).astype(np.float32), "sin": (np.sin(angle) * sign[:, None]).astype(np.float32),
        "key": np.broadcast_to(np.arange(E, 0, -1, dtype=np.float32), (KB, NB, E)),
        "ones8": np.ones((E, C), np.float32), "vecs": np.stack(vecs, 1),
        "b1": p["L0_ffn_b1"].reshape(E * FB, C).T,
        "q0": wq, "qp0": wq[:, turned], "k0": wk, "kp0": wk[:, turned], "v0": wv,
        "q1": p["L0_ffn_Wq"], "k1": p["L0_ffn_Wk"], "v1": p["L0_ffn_Wv"],
        "bv0": rows(bv), "bv1": rows(p["L0_ffn_bv"]),
        "o0": heads(p["L0_attn_out_w"].T), "o1": heads(p["L0_ffn_Wo"]),
        "gate_w": p["L0_ffn_gate_W"], "gate_b": np.broadcast_to(p["L0_ffn_gate_b"], (KB, NB, E)),
        "w1": p["L0_ffn_W1"].transpose(1, 0, 2).reshape(C, E * FF),
        "w2": p["L0_ffn_W2"].reshape(E * FB, C, C).transpose(1, 0, 2), "b2": p["L0_ffn_b2"],
    }
    w_conv = p["L0_tok_W"].reshape(C, C, TAPS).transpose(1, 2, 0)
    sel_rows = np.repeat(np.eye(E, dtype=np.float32), C, axis=1)
    return w_conv, sel_rows, consts


def kernel(**inputs):
    import concourse.bacc as _bacc
    from concourse.bass_utils import run_bass_kernel_spmd as _run

    p = {k: np.asarray(v) for k, v in inputs.items()}
    w_conv, sel_rows, consts = layouts(p)
    arrays = {"x": p["x"], "w_conv": w_conv, "sel_rows": sel_rows, **{f"c_{k}": v for k, v in consts.items()}}
    arrays = {k: np.ascontiguousarray(v) for k, v in arrays.items()}
    nc = _bacc.Bacc("TRN2", target_bir_lowering=False, num_devices=1)
    ap = {k: nc.dram_tensor(k, v.shape, mybir.dt.from_np(v.dtype), kind="ExternalInput").ap() for k, v in arrays.items()}
    out = nc.dram_tensor("out", (B, C, L), F32, kind="ExternalOutput").ap()
    build(nc, ap["x"], ap["w_conv"], ap["sel_rows"], {k: ap[f"c_{k}"] for k in LOADS}, out)
    r = _run(nc, [arrays], core_ids=[0])
    return np.ascontiguousarray(r.results[0]["out"].transpose(0, 2, 1))
```
